# Optimizing a Trainium2 kernel written in Bass

```python
import numpy as np
import jax
import jax.numpy as jnp

def _softmax(x, axis=-1):
    return jax.nn.softmax(x, axis=axis)

def _gelu(x):
    return jax.nn.gelu(x, approximate=True)

def _silu(x):
    return jax.nn.silu(x)

def _sigmoid(x):
    return jax.nn.sigmoid(x)

def _layernorm(x, axis=-1, eps=1e-05):
    m = jnp.mean(x, axis=axis, keepdims=True)
    v = jnp.var(x, axis=axis, keepdims=True)
    return (x - m) / jnp.sqrt(v + eps)

def _scatter_add(tgt, idx, src, axis=0):
    return tgt.at[idx].add(src)

def _segment_sum(src, seg, n):
    return jax.ops.segment_sum(src, seg, n)
kernel_name = 'mk_adaln_ffn_d2_seqx_r8_d9a4bb'

def setup_inputs(seed: int=0):
    np.random.seed(seed)
    _w = jnp.asarray

    def _rec_inputs():
        import jax
        import jax.numpy as jnp
        _rk = jax.random.key(seed)
        x = -7.109e-05 + 0.9999 * jax.random.normal(jax.random.fold_in(_rk, 1), (16, 128, 128), jnp.float32)
        _lenS = 128 - jax.random.randint(jax.random.fold_in(_rk, 7), (16,), 0, max(1, 128 // 4) + 1, jnp.int32)
        _lenS2 = 128 - jax.random.randint(jax.random.fold_in(_rk, 8), (16,), 0, max(1, 128 // 4) + 1, jnp.int32)
        itok_B_0_8 = jax.random.randint(jax.random.fold_in(_rk, 11), (16,), 0, 9, jnp.int32)
        itok_B_0_15 = jax.random.randint(jax.random.fold_in(_rk, 12), (16,), 0, 16, jnp.int32)
        return (x, itok_B_0_8, itok_B_0_15)
    x, itok_B_0_8, itok_B_0_15 = _rec_inputs()

    def _L0_cond_setup():
        import jax, jax.numpy as jnp
        import numpy as np
        LN_EPS = 1e-05
        key = jax.random.key(seed)
        ks = jax.random.split(key, 8)
        B, S, H, A, L = (32, 256, 128, 32, 10)
        return {'hidden_states': jax.random.normal(ks[0], (B, S, H), dtype=jnp.float32), 'language_ids': jax.random.randint(ks[1], (B,), 0, L, dtype=jnp.int64), 'W1': jax.random.normal(ks[2], (L, H, A), dtype=jnp.float32) * (1.0 / np.sqrt(H)), 'b1': jnp.zeros((L, A), dtype=jnp.float32), 'W2': jax.random.normal(ks[3], (L, A, H), dtype=jnp.float32) * (1.0 / np.sqrt(A)), 'b2': jnp.zeros((L, H), dtype=jnp.float32), 'gamma': jnp.ones((L, H), dtype=jnp.float32), 'beta': jnp.zeros((L, H), dtype=jnp.float32)}
    _L0_cond_all = _L0_cond_setup()
    _L0_cond_in = {k: v for k, v in _L0_cond_all.items() if k in ('W1', 'b1', 'W2', 'b2', 'gamma', 'beta')}
    del _L0_cond_all

    def _L0_ffn_setup():
        import jax, jax.numpy as jnp
        import numpy as np
        DIM = 128
        DEPTH = 2
        HEADS = 8
        DIM_HEAD = 64
        WINDOW = 64
        INNER = HEADS * DIM_HEAD
        HID = int(DIM * 4 * 2 / 3)
        B, N = (2, 1024)
        QK_SCALE = 8.0

        def shift_token(t):
            t1, t2 = jnp.split(t, 2, axis=-1)
            t2 = jnp.pad(t2, ((0, 0), (1, 0), (0, 0)))[:, :-1]
            return jnp.concatenate([t1, t2], axis=-1)

        def l2norm(t):
            return t / jnp.clip(jnp.linalg.norm(t, axis=-1, keepdims=True), 1e-12)

        def rotate_half(x):
            x1, x2 = jnp.split(x, 2, axis=-1)
            return jnp.concatenate([-x2, x1], axis=-1)

        def rotary_xpos(q, k):
            n = q.shape[-2]
            half_idx = jnp.arange(0, DIM_HEAD, 2, dtype=jnp.float32)
            inv_freq = 1.0 / 10000.0 ** (half_idx / DIM_HEAD)
            t = jnp.arange(n, dtype=jnp.float32)
            freqs = t[:, None] * inv_freq[None, :]
            freqs = jnp.concatenate([freqs, freqs], axis=-1)
            base = (half_idx + 0.4 * DIM_HEAD) / (1.4 * DIM_HEAD)
            power = (t - n // 2) / float(WINDOW // 2)
            scale = base[None, :] ** power[:, None]
            scale = jnp.concatenate([scale, scale], axis=-1)
            cos, sin = (jnp.cos(freqs), jnp.sin(freqs))
            q = q * cos * scale + rotate_half(q) * sin * scale
            k = k * cos / scale + rotate_half(k) * sin / scale
            return (q, k)

        def local_attention(q, k, v):
            b, h, n, d = q.shape
            w = n // WINDOW
            bq = q.reshape(b, h, w, WINDOW, d) * QK_SCALE
            bk = k.reshape(b, h, w, WINDOW, d)
            bv = v.reshape(b, h, w, WINDOW, d)

            def look_around(t):
                p = jnp.pad(t, ((0, 0), (0, 0), (1, 0), (0, 0), (0, 0)))
                return jnp.concatenate([p[:, :, :w], p[:, :, 1:]], axis=3)
            bk, bv = (look_around(bk), look_around(bv))
            bt = jnp.arange(n).reshape(w, WINDOW)
            btp = jnp.pad(bt, ((1, 0), (0, 0)), constant_values=-1)
            btk = jnp.concatenate([btp[:w], btp[1:]], axis=1)
            sim = jnp.einsum('bhwid,bhwjd->bhwij', bq, bk)
            i = bt[:, :, None]
            j = btk[:, None, :]
            mask = (i < j) | (i > j + WINDOW) | (j == -1)
            sim = jnp.where(mask, -jnp.finfo(sim.dtype).max, sim)
            attn = jax.nn.softmax(sim, axis=-1)
            out = jnp.einsum('bhwij,bhwjd->bhwid', attn, bv)
            return out.reshape(b, h, n, d)

        def _layer(x, wqkv, qs, ksc, wo, lg, lb, w1, b1, w2, b2):
            b, n, _ = x.shape
            h = shift_token(x)
            qkv = h @ wqkv
            q, k, v = jnp.split(qkv, 3, axis=-1)
            to_heads = lambda t: t.reshape(b, n, HEADS, DIM_HEAD).transpose(0, 2, 1, 3)
            q, k, v = (to_heads(q), to_heads(k), to_heads(v))
            q = l2norm(q) * qs
            k = l2norm(k) * ksc
            q, k = rotary_xpos(q, k)
            o = local_attention(q, k, v)
            o = o.transpose(0, 2, 1, 3).reshape(b, n, INNER)
            x = x + o @ wo
            h = shift_token(x)
            mu = h.mean(-1, keepdims=True)
            var = h.var(-1, keepdims=True)
            h = (h - mu) / jnp.sqrt(var + 1e-05) * lg + lb
            h = h @ w1 + b1
            a, g = jnp.split(h, 2, axis=-1)
            h = a * jax.nn.gelu(g, approximate=False)
            x = x + h @ w2 + b2
            return x
        key = jax.random.key(seed)
        ks = jax.random.split(key, 6)
        return {'x': jax.random.normal(ks[0], (B, N, DIM), jnp.float32), 'wqkv': jax.random.normal(ks[1], (DEPTH, DIM, 3 * INNER), jnp.float32) * 0.02, 'q_scale': jnp.ones((DEPTH, DIM_HEAD), jnp.float32), 'k_scale': jnp.ones((DEPTH, DIM_HEAD), jnp.float32), 'wo': jax.random.normal(ks[2], (DEPTH, INNER, DIM), jnp.float32) * 0.02, 'ln_g': jnp.ones((DEPTH, DIM), jnp.float32), 'ln_b': jnp.zeros((DEPTH, DIM), jnp.float32), 'w1': jax.random.normal(ks[3], (DEPTH, DIM, 2 * HID), jnp.float32) * 0.02, 'b1': jnp.zeros((DEPTH, 2 * HID), jnp.float32), 'w2': jax.random.normal(ks[4], (DEPTH, HID, DIM), jnp.float32) * 0.02, 'b2': jnp.zeros((DEPTH, DIM), jnp.float32)}
    _L0_ffn_all = _L0_ffn_setup()
    _L0_ffn_in = {k: v for k, v in _L0_ffn_all.items() if k in ('wqkv', 'q_scale', 'k_scale', 'wo', 'ln_g', 'ln_b', 'w1', 'b1', 'w2', 'b2')}
    del _L0_ffn_all

    def _L1_cond_setup():
        import jax, jax.numpy as jnp
        import numpy as np
        B, N, C_IN, C_OUT, S = (64, 128, 128, 128, 16)
        key = jax.random.key(seed)
        kx, ks, kw, kb = jax.random.split(key, 4)
        scale = 1.0 / np.sqrt(C_IN)
        x = jax.random.normal(kx, (B, N, C_IN), dtype=jnp.float32)
        subjects = jax.random.randint(ks, (B,), 0, S, dtype=jnp.int64)
        weights = jax.random.normal(kw, (S, C_IN, C_OUT), dtype=jnp.float32) * scale
        b = jax.random.normal(kb, (S, C_OUT), dtype=jnp.float32) * scale
        return {'x': x, 'subjects': subjects, 'weights': weights, 'b': b}
    _L1_cond_all = _L1_cond_setup()
    _L1_cond_in = {k: v for k, v in _L1_cond_all.items() if k in ('weights', 'b')}
    del _L1_cond_all

    def _L1_ffn_setup():
        import jax, jax.numpy as jnp
        import numpy as np
        EPS = 1e-06
        LN_EPS = 1e-05

        def _absmean_core(W):
            gamma = jnp.mean(jnp.abs(W)) + EPS
            Ws = W / gamma
            Wq = jnp.sign(Ws) * jnp.minimum(jnp.round(jnp.abs(Ws)), 1.0)
            return (Wq, gamma)

        @jax.custom_vjp
        def absmean(W):
            return _absmean_core(W)[0]

        def _absmean_fwd(W):
            Wq, gamma = _absmean_core(W)
            return (Wq, gamma)

        def _absmean_bwd(gamma, g):
            return (g / gamma,)
        absmean.defvjp(_absmean_fwd, _absmean_bwd)

        def layernorm(x, w, b, eps=LN_EPS):
            mu = jnp.mean(x, axis=-1, keepdims=True)
            var = jnp.mean((x - mu) ** 2, axis=-1, keepdims=True)
            return (x - mu) * jax.lax.rsqrt(var + eps) * w + b
        key = jax.random.key(seed)
        k1, k2, k3 = jax.random.split(key, 3)
        d, h = (128, 512)
        B, T = (8, 256)
        return {'x': jax.random.normal(k1, (B, T, d), jnp.float32), 'W_fc': jax.random.normal(k2, (h, d), jnp.float32), 'ln_w': jnp.ones((h,), jnp.float32), 'ln_b': jnp.zeros((h,), jnp.float32), 'W_proj': jax.random.normal(k3, (d, h), jnp.float32)}
    _L1_ffn_all = _L1_ffn_setup()
    _L1_ffn_in = {k: v for k, v in _L1_ffn_all.items() if k in ('W_fc', 'ln_w', 'ln_b', 'W_proj')}
    del _L1_ffn_all
    return {'x': x, 'itok_B_0_8': itok_B_0_8, 'itok_B_0_15': itok_B_0_15, 'L0_cond_W1': _L0_cond_in['W1'], 'L0_cond_b1': _L0_cond_in['b1'], 'L0_cond_W2': _L0_cond_in['W2'], 'L0_cond_b2': _L0_cond_in['b2'], 'L0_cond_gamma': _L0_cond_in['gamma'], 'L0_cond_beta': _L0_cond_in['beta'], 'L0_ffn_wqkv': _L0_ffn_in['wqkv'], 'L0_ffn_q_scale': _L0_ffn_in['q_scale'], 'L0_ffn_k_scale': _L0_ffn_in['k_scale'], 'L0_ffn_wo': _L0_ffn_in['wo'], 'L0_ffn_ln_g': _L0_ffn_in['ln_g'], 'L0_ffn_ln_b': _L0_ffn_in['ln_b'], 'L0_ffn_w1': _L0_ffn_in['w1'], 'L0_ffn_b1': _L0_ffn_in['b1'], 'L0_ffn_w2': _L0_ffn_in['w2'], 'L0_ffn_b2': _L0_ffn_in['b2'], 'L1_cond_weights': _L1_cond_in['weights'], 'L1_cond_b': _L1_cond_in['b'], 'L1_ffn_W_fc': _L1_ffn_in['W_fc'], 'L1_ffn_ln_w': _L1_ffn_in['ln_w'], 'L1_ffn_ln_b': _L1_ffn_in['ln_b'], 'L1_ffn_W_proj': _L1_ffn_in['W_proj']}

def reference(x, itok_B_0_8, itok_B_0_15, L0_cond_W1, L0_cond_b1, L0_cond_W2, L0_cond_b2, L0_cond_gamma, L0_cond_beta, L0_ffn_wqkv, L0_ffn_q_scale, L0_ffn_k_scale, L0_ffn_wo, L0_ffn_ln_g, L0_ffn_ln_b, L0_ffn_w1, L0_ffn_b1, L0_ffn_w2, L0_ffn_b2, L1_cond_weights, L1_cond_b, L1_ffn_W_fc, L1_ffn_ln_w, L1_ffn_ln_b, L1_ffn_W_proj):
    import jax
    import jax.numpy as jnp

    def _L0_cond_ref(hidden_states, language_ids, W1, b1, W2, b2, gamma, beta):
        import jax, jax.numpy as jnp
        import numpy as np
        LN_EPS = 1e-05
        w1 = W1[language_ids]
        w2 = W2[language_ids]
        h = jnp.einsum('bsh,bha->bsa', hidden_states, w1) + b1[language_ids][:, None, :]
        h = jax.nn.relu(h)
        adapted = jnp.einsum('bsa,bah->bsh', h, w2) + b2[language_ids][:, None, :]
        x = hidden_states + adapted
        mean = jnp.mean(x, axis=-1, keepdims=True)
        var = jnp.mean(jnp.square(x - mean), axis=-1, keepdims=True)
        normed = (x - mean) * jax.lax.rsqrt(var + LN_EPS)
        return normed * gamma[language_ids][:, None, :] + beta[language_ids][:, None, :]

    def _L0_ffn_ref(x, wqkv, q_scale, k_scale, wo, ln_g, ln_b, w1, b1, w2, b2):
        import jax, jax.numpy as jnp
        import numpy as np
        DIM = 128
        DEPTH = 2
        HEADS = 8
        DIM_HEAD = 64
        WINDOW = 64
        INNER = HEADS * DIM_HEAD
        HID = int(DIM * 4 * 2 / 3)
        B, N = (2, 1024)
        QK_SCALE = 8.0

        def shift_token(t):
            t1, t2 = jnp.split(t, 2, axis=-1)
            t2 = jnp.pad(t2, ((0, 0), (1, 0), (0, 0)))[:, :-1]
            return jnp.concatenate([t1, t2], axis=-1)

        def l2norm(t):
            return t / jnp.clip(jnp.linalg.norm(t, axis=-1, keepdims=True), 1e-12)

        def rotate_half(x):
            x1, x2 = jnp.split(x, 2, axis=-1)
            return jnp.concatenate([-x2, x1], axis=-1)

        def rotary_xpos(q, k):
            n = q.shape[-2]
            half_idx = jnp.arange(0, DIM_HEAD, 2, dtype=jnp.float32)
            inv_freq = 1.0 / 10000.0 ** (half_idx / DIM_HEAD)
            t = jnp.arange(n, dtype=jnp.float32)
            freqs = t[:, None] * inv_freq[None, :]
            freqs = jnp.concatenate([freqs, freqs], axis=-1)
            base = (half_idx + 0.4 * DIM_HEAD) / (1.4 * DIM_HEAD)
            power = (t - n // 2) / float(WINDOW // 2)
            scale = base[None, :] ** power[:, None]
            scale = jnp.concatenate([scale, scale], axis=-1)
            cos, sin = (jnp.cos(freqs), jnp.sin(freqs))
            q = q * cos * scale + rotate_half(q) * sin * scale
            k = k * cos / scale + rotate_half(k) * sin / scale
            return (q, k)

        def local_attention(q, k, v):
            b, h, n, d = q.shape
            w = n // WINDOW
            bq = q.reshape(b, h, w, WINDOW, d) * QK_SCALE
            bk = k.reshape(b, h, w, WINDOW, d)
            bv = v.reshape(b, h, w, WINDOW, d)

            def look_around(t):
                p = jnp.pad(t, ((0, 0), (0, 0), (1, 0), (0, 0), (0, 0)))
                return jnp.concatenate([p[:, :, :w], p[:, :, 1:]], axis=3)
            bk, bv = (look_around(bk), look_around(bv))
            bt = jnp.arange(n).reshape(w, WINDOW)
            btp = jnp.pad(bt, ((1, 0), (0, 0)), constant_values=-1)
            btk = jnp.concatenate([btp[:w], btp[1:]], axis=1)
            sim = jnp.einsum('bhwid,bhwjd->bhwij', bq, bk)
            i = bt[:, :, None]
            j = btk[:, None, :]
            mask = (i < j) | (i > j + WINDOW) | (j == -1)
            sim = jnp.where(mask, -jnp.finfo(sim.dtype).max, sim)
            attn = jax.nn.softmax(sim, axis=-1)
            out = jnp.einsum('bhwij,bhwjd->bhwid', attn, bv)
            return out.reshape(b, h, n, d)

        def _layer(x, wqkv, qs, ksc, wo, lg, lb, w1, b1, w2, b2):
            b, n, _ = x.shape
            h = shift_token(x)
            qkv = h @ wqkv
            q, k, v = jnp.split(qkv, 3, axis=-1)
            to_heads = lambda t: t.reshape(b, n, HEADS, DIM_HEAD).transpose(0, 2, 1, 3)
            q, k, v = (to_heads(q), to_heads(k), to_heads(v))
            q = l2norm(q) * qs
            k = l2norm(k) * ksc
            q, k = rotary_xpos(q, k)
            o = local_attention(q, k, v)
            o = o.transpose(0, 2, 1, 3).reshape(b, n, INNER)
            x = x + o @ wo
            h = shift_token(x)
            mu = h.mean(-1, keepdims=True)
            var = h.var(-1, keepdims=True)
            h = (h - mu) / jnp.sqrt(var + 1e-05) * lg + lb
            h = h @ w1 + b1
            a, g = jnp.split(h, 2, axis=-1)
            h = a * jax.nn.gelu(g, approximate=False)
            x = x + h @ w2 + b2
            return x
        for l in range(DEPTH):
            x = _layer(x, wqkv[l], q_scale[l], k_scale[l], wo[l], ln_g[l], ln_b[l], w1[l], b1[l], w2[l], b2[l])
        return x

    def _L1_cond_ref(x, subjects, weights, b):
        import jax, jax.numpy as jnp
        import numpy as np
        B, N, C_IN, C_OUT, S = (64, 128, 128, 128, 16)
        w = weights[subjects]
        out = jnp.einsum('bnc,bcd->bnd', x, w)
        out = out + b[subjects][:, None, :]
        return out

    def _L1_ffn_ref(x, W_fc, ln_w, ln_b, W_proj):
        import jax, jax.numpy as jnp
        import numpy as np
        EPS = 1e-06
        LN_EPS = 1e-05

        def _absmean_core(W):
            gamma = jnp.mean(jnp.abs(W)) + EPS
            Ws = W / gamma
            Wq = jnp.sign(Ws) * jnp.minimum(jnp.round(jnp.abs(Ws)), 1.0)
            return (Wq, gamma)

        @jax.custom_vjp
        def absmean(W):
            return _absmean_core(W)[0]

        def _absmean_fwd(W):
            Wq, gamma = _absmean_core(W)
            return (Wq, gamma)

        def _absmean_bwd(gamma, g):
            return (g / gamma,)
        absmean.defvjp(_absmean_fwd, _absmean_bwd)

        def layernorm(x, w, b, eps=LN_EPS):
            mu = jnp.mean(x, axis=-1, keepdims=True)
            var = jnp.mean((x - mu) ** 2, axis=-1, keepdims=True)
            return (x - mu) * jax.lax.rsqrt(var + eps) * w + b
        h = jnp.einsum('btd,hd->bth', x, absmean(W_fc))
        h = jax.nn.gelu(h, approximate=False)
        h = layernorm(h, ln_w, ln_b)
        return jnp.einsum('bth,dh->btd', h, absmean(W_proj))
    x = x + _L0_ffn_ref(_L0_cond_ref(x, itok_B_0_8, L0_cond_W1, L0_cond_b1, L0_cond_W2, L0_cond_b2, L0_cond_gamma, L0_cond_beta), L0_ffn_wqkv, L0_ffn_q_scale, L0_ffn_k_scale, L0_ffn_wo, L0_ffn_ln_g, L0_ffn_ln_b, L0_ffn_w1, L0_ffn_b1, L0_ffn_w2, L0_ffn_b2)
    x = x + _L1_ffn_ref(_L1_cond_ref(x, itok_B_0_15, L1_cond_weights, L1_cond_b), L1_ffn_W_fc, L1_ffn_ln_w, L1_ffn_ln_b, L1_ffn_W_proj)
    return x

_drawn_inputs = setup_inputs


def setup_inputs(seed=0):
    import zlib

    import numpy as np

    out = dict(_drawn_inputs(seed))
    spreads = {'L0_cond_b1': (0.0, 0.1),
     'L0_cond_b2': (0.0, 0.1),
     'L0_cond_gamma': (1.0, 0.2),
     'L0_cond_beta': (0.0, 0.1),
     'L0_ffn_q_scale': (1.0, 0.6),
     'L0_ffn_k_scale': (1.0, 0.6),
     'L0_ffn_ln_g': (1.0, 0.6),
     'L0_ffn_ln_b': (0.0, 0.8),
     'L0_ffn_b1': (0.0, 0.8),
     'L0_ffn_b2': (0.0, 0.1),
     'L1_ffn_ln_w': (1.0, 0.2),
     'L1_ffn_ln_b': (0.0, 0.1)}
    factors = {'L0_ffn_w1': 4.911, 'L0_ffn_w2': 4.843, 'L1_cond_b': 4.072}
    for name, (base, spread) in spreads.items():
        noise = np.random.default_rng([zlib.crc32(name.encode()), seed]).standard_normal(out[name].shape)
        drawn = base * np.exp(spread * noise) if base else spread * noise
        out[name] = jnp.asarray(drawn.astype(out[name].dtype))
    for name, factor in factors.items():
        out[name] = (out[name] * factor).astype(out[name].dtype)
    return out
```

```python
from contextlib import ExitStack

import numpy as np

import concourse.bass as bass
from concourse import mybir

F32 = mybir.dt.float32
BF16 = mybir.dt.bfloat16
I32 = mybir.dt.int32
ACT = mybir.ActivationFunctionType
ALU = mybir.AluOpType
AX = mybir.AxisListType

P = 128
SEQS, TOK, DIM = 16, 128, 128
HALF = DIM // 2
HEADS, HD = 8, 64
INNER = HEADS * HD
DEPTH = 2
HID = int(DIM * 4 * 2 / 3)
NCH = 3
CH = -(-HID // NCH)
CHUNKS = [(c * CH, min(CH, HID - c * CH)) for c in range(NCH)]
ADIM = 32
FC = 512
GSEQ = 4
GROUPS = SEQS // GSEQ
GTOK = GSEQ * TOK
SKEW = 130
WINDOW = 64
QK_SCALE = 8.0
LN_EPS = 1e-5
RSQRT_MAGIC = float(0x5F3759DF)
NEWTON = 3
RSQRT_OPS = 1 + 3 * NEWTON


class Chain:

    def __init__(self, eng, sem, base):
        self.eng, self.sem, self.base, self.n = eng, sem, base, 0

    def add(self, instruction):
        instruction.then_inc(self.sem, 1)
        self.n += 1

    def wait(self):
        self.eng.wait_ge(self.sem, self.base + self.n)


def rsqrt(vec, chain, x, y, t):
    chain.add(vec.tensor_scalar(y.bitcast(I32), x.bitcast(I32), -0.5, RSQRT_MAGIC, ALU.mult, ALU.add))
    for _ in range(NEWTON):
        chain.wait()
        chain.add(vec.tensor_tensor(t, y, y, ALU.mult))
        chain.wait()
        chain.add(vec.scalar_tensor_tensor(out=t, in0=t, scalar=-0.5, in1=x, op0=ALU.mult, op1=ALU.mult))
        chain.wait()
        chain.add(vec.scalar_tensor_tensor(out=y, in0=t, scalar=1.5, in1=y, op0=ALU.add, op1=ALU.mult))
    chain.wait()


def at_least(eng, sem, value):
    if not isinstance(value, int) or value > 0:
        eng.wait_ge(sem, value)


class Memory:

    def __init__(self, nc, ctx):
        def sb(name, shape, dt=F32):
            return ctx.enter_context(nc.sbuf_tensor(name, shape, dt))

        self.bank = ctx.enter_context(nc.psum_tensor("bank", [P, 8, 512], F32))
        self.ident = sb("ident", [P, P])
        self.ident16 = sb("ident16", [P, P], BF16)
        self.mask16 = sb("mask16", [P, 4, TOK], BF16)
        self.mask = sb("mask", [P, TOK])
        self.rope = sb("rope", [P, 2, 2, HD])
        self.ones = sb("ones", [P, P])
        self.x_in = sb("x_in", [P, SEQS, DIM])
        self.xT = sb("xT", [P, SEQS, TOK])
        self.res = sb("res", [P, SEQS, SKEW])
        self.x1T = sb("x1T", [P, SEQS, TOK])
        self.idx = sb("idx", [1, 2, SEQS], I32)
        self.id8 = sb("id8", [10, SEQS], I32)
        self.id15 = sb("id15", [16, SEQS], I32)
        self.hot8 = sb("hot8", [10, SEQS])
        self.hot15 = sb("hot15", [16, SEQS])
        self.part = sb("part", [16, 1])
        self.rows8 = sb("rows8", [10, ADIM + 2 * DIM])
        self.rows15 = sb("rows15", [16, DIM])
        self.b1T = sb("b1T", [ADIM, SEQS])
        self.gammaT = sb("gammaT", [P, SEQS])
        self.betaT = sb("betaT", [P, SEQS])
        self.bcT = sb("bcT", [P, SEQS])
        self.cw1 = sb("cw1", [P, GSEQ, ADIM])
        self.cw2 = sb("cw2", [ADIM + 1, SEQS, DIM])
        self.cwc = sb("cwc", [P, GSEQ, DIM])
        self.wqkv = sb("wqkv", [P, DEPTH, 3 * INNER])
        self.wo = sb("wo", [P, DEPTH, INNER // P, DIM])
        self.w1 = sb("w1", [P, DEPTH, 2 * HID])
        self.w2 = sb("w2", [CH, DEPTH, NCH, DIM])
        self.b1 = sb("b1", [CH, DEPTH, 2 * NCH])
        self.b1eff = sb("b1eff", [CH, DEPTH, 2 * NCH])
        self.cols = sb("cols", [P, 3, DEPTH])
        self.qks = sb("qks", [P, DEPTH, 2, HD])
        self.tab = sb("tab", [P, DEPTH, 2, 2, HD])
        self.wf = sb("wf", [P, 2, FC])
        self.wneg = sb("wneg", [P, 2, FC])
        self.wfT = sb("wfT", [P, FC])
        self.wpT = sb("wpT", [P, FC // P, DIM])
        self.ln1 = sb("ln1", [P, 2, FC // P])
        self.absum = sb("absum", [P, 2])
        self.thr = sb("thr", [P, 2])


def prepare(nc, m, a):
    with ExitStack() as ctx:
        sem = lambda name: ctx.enter_context(nc.semaphore(name))
        x_loaded, const_loaded, cond_loaded, l1_loaded, l0_loaded = (
            sem(s) for s in ("x_loaded", "const_loaded", "cond_loaded", "l1_loaded", "l0_loaded"))
        filled, hot_ready, cond_mm, sums, sum_all = (
            sem(s) for s in ("filled", "hot_ready", "cond_mm", "sums", "sum_all"))
        steps, ternary, turned, b1_mm = (sem(s) for s in ("steps", "ternary", "turned", "b1_mm"))
        block = ctx.enter_context(nc.Block())

        @block.sync
        def _(sp):
            sp.dma_start(m.idx[:, 0, :], a["id8"].rearrange("(o s) -> o s", o=1)).then_inc(cond_loaded, 16)
            sp.dma_start(m.idx[:, 1, :], a["id15"].rearrange("(o s) -> o s", o=1)).then_inc(cond_loaded, 16)
            sp.dma_start(m.id8[:, :], a["id8"].partition_broadcast(10)).then_inc(cond_loaded, 16)
            sp.dma_start(m.id15[:, :], a["id15"].partition_broadcast(16)).then_inc(cond_loaded, 16)
            sp.dma_start(m.rows8[:, :], a["rows8"]).then_inc(cond_loaded, 16)
            sp.dma_start(m.rows15[:, :], a["rows15"]).then_inc(cond_loaded, 16)
            sp.dma_start(m.part[:, :], a["part"]).then_inc(cond_loaded, 16)
            sp.dma_start(m.x_in[:, :, :], a["x"].rearrange("s t d -> t s d")).then_inc(x_loaded, 16)
            sp.dma_start(m.wqkv[:, :, :], a["wqkv"].rearrange("l p n -> p l n")).then_inc(l0_loaded, 16)
            sp.dma_start(m.w1[:, :, :], a["w1"].rearrange("l p n -> p l n")).then_inc(l0_loaded, 16)
            sp.dma_start(m.wo[:, :, :, :], a["wo"].rearrange("l (c p) n -> p l c n", p=P)).then_inc(l0_loaded, 16)
            for c, (at, n) in enumerate(CHUNKS):
                sp.dma_start(m.w2[0:n, :, c, :], a["w2"][:, at:at + n, :].rearrange("l p n -> p l n"))\
                    .then_inc(l0_loaded, 16)
                for half in range(2):
                    sp.dma_start(m.b1[0:n, :, half * NCH + c],
                                 a["b1"][:, half * HID + at:half * HID + at + n].rearrange("l p -> p l"),
                                 allow_slow_non_contiguous=True).then_inc(l0_loaded, 16)
            sp.wait_ge(x_loaded, 16)
            sp.wait_ge(l0_loaded, 16 * (3 + 3 * NCH))

        @block.scalar
        def _(act):
            for dst, name in ((m.ident[:, :], "ident"), (m.mask[:, :], "mask"),
                              (m.rope[:, :, :, :], "rope")):
                act.dma_start(dst, a[name]).then_inc(const_loaded, 16)
            act.dma_start(m.wf[:, 0, :].rearrange("p (c n) -> p c n", c=4),
                          a["W_fc"].rearrange("(c p) n -> p c n", p=P)).then_inc(l1_loaded, 16)
            act.dma_start(m.wf[:, 1, :], a["W_proj"]).then_inc(l1_loaded, 16)
            for k, name in enumerate(("ln_w", "ln_b")):
                act.dma_start(m.ln1[:, k, :], a[name].rearrange("(c p) -> p c", p=P),
                              allow_slow_non_contiguous=True).then_inc(l1_loaded, 16)
            for k, name in enumerate(("ln_g0", "ln_b0", "b2")):
                act.dma_start(m.cols[:, k, :], a[name].rearrange("l p -> p l"),
                              allow_slow_non_contiguous=True).then_inc(const_loaded, 16)
            act.dma_start(m.qks[:, :, :, :].rearrange("p l t d -> p (l t d)"),
                          a["qks"].partition_broadcast(P)).then_inc(const_loaded, 16)
            act.wait_ge(const_loaded, 16 * 7)
            act.wait_ge(l1_loaded, 16 * 4)

        @block.gpsimd
        def _(pool):
            pool.memset(m.ones[:, :], 1.0).then_inc(filled, 1)
            pool.memset(m.res[:, :, :], 0.0).then_inc(filled, 1)

        @block.tensor
        def _(pe):
            pe.wait_ge(hot_ready, 2)
            pe.matmul(m.bank[0:ADIM, 0, 0:SEQS], m.rows8[:, 0:ADIM], m.hot8[:, :], start=True, stop=True)
            pe.matmul(m.bank[:, 1, 0:SEQS], m.rows8[:, ADIM:ADIM + DIM], m.hot8[:, :], start=True, stop=True)
            pe.matmul(m.bank[:, 2, 0:SEQS], m.rows8[:, ADIM + DIM:], m.hot8[:, :], start=True, stop=True)
            pe.matmul(m.bank[:, 3, 0:SEQS], m.rows15[:, :], m.hot15[:, :], start=True, stop=True)\
                .then_inc(cond_mm, 1)
            pe.wait_ge(filled, 1)
            pe.wait_ge(sums, 2)
            pe.matmul(m.bank[:, 4, 0:2], m.ones[:, :], m.absum[:, :], start=True, stop=True).then_inc(sum_all, 1)
            pe.wait_ge(l0_loaded, 16 * (3 + 3 * NCH))
            pe.wait_ge(const_loaded, 16 * 7)
            for layer in range(DEPTH):
                for k in range(2 * NCH):
                    at, n = CHUNKS[k % NCH]
                    at += (k // NCH) * HID
                    mm = pe.matmul(m.bank[0:n, 5, layer * 2 * NCH + k:layer * 2 * NCH + k + 1],
                                   m.w1[:, layer, at:at + n], m.cols[:, 1, layer:layer + 1],
                                   start=True, stop=True)
            mm.then_inc(b1_mm, 1)
            pe.wait_ge(ternary, 1)
            for c in range(4):
                pe.transpose(m.bank[:, 6, c * P:(c + 1) * P], m.wf[:, 0, c * P:(c + 1) * P], m.ident[:, :])
            for c in range(4):
                mm = pe.transpose(m.bank[:, 7, c * P:(c + 1) * P], m.wf[:, 1, c * P:(c + 1) * P], m.ident[:, :])
            mm.then_inc(turned, 1)

        @block.vector
        def _(dve):
            vec = nc.vector
            chain = Chain(dve, steps, 0)
            dve.wait_ge(cond_loaded, 16 * 7)
            vec.tensor_scalar(m.hot8[:, :], m.id8[:, :], m.part[0:10, :], None, ALU.is_equal).then_inc(hot_ready, 1)
            vec.tensor_scalar(m.hot15[:, :], m.id15[:, :], m.part[:, :], None, ALU.is_equal).then_inc(hot_ready, 1)
            dve.wait_ge(cond_mm, 1)
            vec.tensor_copy(m.b1T[:, :], m.bank[0:ADIM, 0, 0:SEQS])
            vec.tensor_copy(m.gammaT[:, :], m.bank[:, 1, 0:SEQS])
            vec.tensor_copy(m.betaT[:, :], m.bank[:, 2, 0:SEQS])
            vec.tensor_copy(m.bcT[:, :], m.bank[:, 3, 0:SEQS])
            dve.wait_ge(const_loaded, 16 * 7)
            vec.tensor_copy(m.ident16[:, :], m.ident[:, :])
            vec.tensor_copy(m.mask16[:, :, :], m.mask[:, :].unsqueeze(1).broadcast_to([P, 4, TOK]))
            for layer in range(DEPTH):
                for k in range(2):
                    vec.tensor_tensor(m.tab[:, layer, k, :, :], m.rope[:, k, :, :], m.qks[:, layer, :, :], ALU.mult)
            dve.wait_ge(l1_loaded, 16 * 4)
            for k in range(2):
                vec.tensor_reduce(m.absum[:, k:k + 1], m.wf[:, k, :], AX.X, ALU.add, apply_absolute_value=True)\
                    .then_inc(sums, 1)
            dve.wait_ge(sum_all, 1)
            chain.add(vec.tensor_scalar(m.thr[:, :], m.bank[:, 4, 0:2], 1.0 / (FC * DIM), 1e-6, ALU.mult, ALU.add))
            chain.wait()
            chain.add(vec.tensor_scalar(m.thr[:, :], m.thr[:, :], 0.5, None, ALU.mult))
            chain.wait()
            for k in range(2):
                chain.add(vec.tensor_scalar(m.wneg[:, k, :], m.wf[:, k, :], -1.0, m.thr[:, k:k + 1],
                                            ALU.mult, ALU.is_gt))
            chain.wait()
            for k in range(2):
                last = vec.scalar_tensor_tensor(out=m.wf[:, k, :], in0=m.wf[:, k, :], scalar=m.thr[:, k:k + 1],
                                                in1=m.wneg[:, k, :], op0=ALU.is_gt, op1=ALU.subtract)
            last.then_inc(ternary, 1)
            dve.wait_ge(b1_mm, 1)
            for layer in range(DEPTH):
                for k in range(2 * NCH):
                    n = CHUNKS[k % NCH][1]
                    vec.tensor_tensor(m.b1eff[0:n, layer, k:k + 1],
                                      m.bank[0:n, 5, layer * 2 * NCH + k:layer * 2 * NCH + k + 1],
                                      m.b1[0:n, layer, k:k + 1], ALU.add)
                vec.tensor_scalar(m.w1[:, layer, :], m.w1[:, layer, :], m.cols[:, 0, layer:layer + 1], None, ALU.mult)
            dve.wait_ge(turned, 1)
            vec.tensor_copy(m.wfT[:, :], m.bank[:, 6, :])
            vec.tensor_copy(m.wpT[:, :, :].rearrange("p c n -> p (c n)"), m.bank[:, 7, :])


def conditioned_adapter(nc, m, a):
    with ExitStack() as ctx:
        sem = lambda name: ctx.enter_context(nc.semaphore(name))
        sb = lambda name, shape: ctx.enter_context(nc.sbuf_tensor(name, shape, F32))
        w_loaded, w2_loaded, xt_mm, xt_sb, h1_mm, h1_sb = (
            sem(s) for s in ("w_loaded", "w2_loaded", "xt_mm", "xt_sb", "h1_mm", "h1_sb"))
        ad_mm, xn_sb, xn_mm, res_sb, steps, one_row, sum_sb = (
            sem(s) for s in ("ad_mm", "xn_sb", "xn_mm", "res_sb", "cond_steps", "one_row", "sum_sb"))
        h1 = sb("h1", [ADIM + 1, GSEQ, TOK])
        xr = sb("xr", [P, GSEQ, DIM])
        xn = sb("xn", [P, GSEQ, DIM])
        stats = sb("c_stats", [P, GSEQ, 6])
        mv = sb("c_mv", [P, GSEQ, 2])
        ve = sb("c_ve", [P, GSEQ])
        rstd = sb("c_rstd", [P, GSEQ])
        tmp = sb("c_tmp", [P, GSEQ])
        PX, PH, PA, PN = 0, 1, 2, 3
        block = ctx.enter_context(nc.Block())

        @block.sync
        def _(sp):
            with sp.Fori(0, SEQS) as s:
                lang = sp.value_load(m.idx[0:1, 0, bass.ds(s, 1)], min_val=0, max_val=9)
                sp.dma_start(m.cw2[:, bass.ds(s, 1), :],
                             a["cw2"][bass.ds(lang, 1), :, :].rearrange("o p n -> p o n")).then_inc(w2_loaded, 16)
            sp.wait_ge(w2_loaded, 16 * SEQS)

        @block.gpsimd
        def _(pool):
            pool.memset(h1[ADIM:ADIM + 1, :, :], 1.0).then_inc(one_row, 1)

        @block.tensor
        def _(pe):
            pe.wait_ge(one_row, 1)
            for g in range(GROUPS):
                at_least(pe, xt_sb, g)
                for j in range(GSEQ):
                    mm = pe.transpose(m.bank[:, PX, j * P:(j + 1) * P], m.x_in[:, GSEQ * g + j, :], m.ident[:, :])
                mm.then_inc(xt_mm, 1)
                pe.wait_ge(xt_sb, g + 1)
                pe.wait_ge(w_loaded, 16 * GSEQ * (g + 1))
                at_least(pe, h1_sb, g)
                for j in range(GSEQ):
                    mm = pe.matmul(m.bank[0:ADIM, PH, j * P:(j + 1) * P], m.cw1[:, j, :],
                                   m.xT[:, GSEQ * g + j, :], start=True, stop=True)
                mm.then_inc(h1_mm, 1)
                pe.wait_ge(h1_sb, g + 1)
                if g == 0:
                    pe.wait_ge(w2_loaded, 16 * SEQS)
                at_least(pe, sum_sb, g)
                for j in range(GSEQ):
                    mm = pe.matmul(m.bank[:, PA, j * P:(j + 1) * P], h1[:, j, :],
                                   m.cw2[:, GSEQ * g + j, :], start=True, stop=True)
                mm.then_inc(ad_mm, 1)
                pe.wait_ge(xn_sb, g + 1)
                at_least(pe, res_sb, g)
                for j in range(GSEQ):
                    mm = pe.transpose(m.bank[:, PN, j * P:(j + 1) * P], xn[:, j, :], m.ident[:, :])
                mm.then_inc(xn_mm, 1)

        @block.scalar
        def _(act):
            for g in range(GROUPS):
                at_least(act, h1_mm, g)
                for j in range(GSEQ):
                    lang = act.value_load(m.idx[0:1, 0, GSEQ * g + j:GSEQ * g + j + 1], min_val=0, max_val=9)
                    act.dma_start(m.cw1[:, j:j + 1, :],
                                  a["cw1"][bass.ds(lang, 1), :, :].rearrange("o p n -> p o n"))\
                        .then_inc(w_loaded, 16)
                act.wait_ge(xt_mm, g + 1)
                act.copy(m.xT[:, GSEQ * g:GSEQ * (g + 1), :].rearrange("p s t -> p (s t)"), m.bank[:, PX, :])\
                    .then_inc(xt_sb, 1)
                act.wait_ge(h1_mm, g + 1)
                at_least(act, ad_mm, g)
                for j in range(GSEQ):
                    s = GSEQ * g + j
                    last = act.activation(h1[0:ADIM, j, :], m.bank[0:ADIM, PH, j * P:(j + 1) * P], ACT.Relu,
                                          bias=m.b1T[:, s:s + 1])
                last.then_inc(h1_sb, 1)
            act.wait_ge(w_loaded, 16 * SEQS)

        @block.vector
        def _(dve):
            vec = nc.vector
            chain = Chain(dve, steps, 0)
            for g in range(GROUPS):
                dve.wait_ge(ad_mm, g + 1)
                vec.tensor_tensor(xr[:, :, :].rearrange("p s t -> p (s t)"), m.bank[:, PA, :],
                                  m.x_in[:, GSEQ * g:GSEQ * (g + 1), :].rearrange("p s t -> p (s t)"), ALU.add)\
                    .then_inc(sum_sb, 1)
                dve.wait_ge(sum_sb, g + 1)
                layernorm_stats(vec, chain, xr, stats, mv, ve, rstd, tmp, DIM)
                at_least(dve, xn_mm, g)
                for j in range(GSEQ):
                    last = vec.tensor_scalar(xn[:, j, :], xr[:, j, :], mv[:, j, 0:1], rstd[:, j:j + 1],
                                             ALU.subtract, ALU.mult)
                last.then_inc(xn_sb, 1)
                dve.wait_ge(xn_mm, g + 1)
                for j in range(GSEQ):
                    s = GSEQ * g + j
                    for k in range(2):
                        rows = slice(k * HALF, (k + 1) * HALF)
                        last = vec.tensor_scalar(m.res[rows, s, k:k + TOK], m.bank[rows, PN, j * P:(j + 1) * P],
                                                 m.gammaT[rows, s:s + 1], m.betaT[rows, s:s + 1],
                                                 ALU.mult, ALU.add)
                last.then_inc(res_sb, 1)


def layernorm_stats(vec, chain, rows, stats, mv, ve, rstd, tmp, width):
    for j in range(GSEQ):
        chain.add(vec.bn_stats(stats[:, j, :], rows[:, j, :]))
    chain.wait()
    (me, qe), (mo, qo) = ((stats[:, :, 3 * k + 1], stats[:, :, 3 * k + 2]) for k in range(2))
    chain.add(vec.tensor_tensor(mv[:, :, 0], me, mo, ALU.add))
    chain.add(vec.tensor_tensor(tmp[:, :], me, mo, ALU.subtract))
    chain.add(vec.tensor_tensor(ve[:, :], qe, qo, ALU.add))
    chain.wait()
    chain.add(vec.tensor_scalar(mv[:, :, 0], mv[:, :, 0], 0.5, None, ALU.mult))
    chain.add(vec.scalar_tensor_tensor(out=tmp[:, :], in0=tmp[:, :], scalar=0.25, in1=tmp[:, :],
                                       op0=ALU.mult, op1=ALU.mult))
    chain.add(vec.tensor_scalar(ve[:, :], ve[:, :], 1.0 / width, LN_EPS, ALU.mult, ALU.add))
    chain.wait()
    chain.add(vec.tensor_tensor(ve[:, :], ve[:, :], tmp[:, :], ALU.add))
    chain.wait()
    rsqrt(vec, chain, ve[:, :], rstd[:, :], tmp[:, :])


LN_STEPS = GSEQ + 7 + RSQRT_OPS


def attention(nc, m, layer):
    with ExitStack() as ctx:
        sem = lambda name: ctx.enter_context(nc.semaphore(f"{name}{layer}"))
        sb = lambda name, shape: ctx.enter_context(nc.sbuf_tensor(f"{name}{layer}", shape, F32))
        front_staged, value_staged, qk_mm, v_mm, v_sb = (
            sem(s) for s in ("front_staged", "value_staged", "qk_mm", "v_mm", "v_sb"))
        square_sb, rope_k, norm_ready, rotated, turn_mm, q_sb, k_sb = (
            sem(s) for s in ("square_sb", "rope_k", "norm_ready", "rotated", "turn_mm", "q_sb", "k_sb"))
        score_mm, shift_ready, prob_sb, inv_ready, prob_ok, probT_mm, probTa_sb, probTb_sb = (
            sem(s) for s in ("score_mm", "shift_ready", "prob_sb", "inv_ready", "prob_ok", "probT_mm",
                             "probTa_sb", "probTb_sb"))
        out_mm, out_sb, y_mm, res_ok, norm_steps, max_steps, pool_steps = (
            sem(s) for s in ("out_mm", "out_sb", "y_mm", "res_ok", "norm_steps", "max_steps", "pool_steps"))

        hf = sb("hf", [P, TOK])
        hv = sb("hv", [P, TOK])
        v = sb("v", [P, INNER])
        sq = sb("sq", [P, 2 * HEADS, HD])
        ta = sb("ta", [P, 2 * HEADS, HD])
        tb = sb("tb", [P, 2 * HEADS, HD])
        rot = sb("rot", [P, 2 * HEADS, HD])
        ssq = sb("ssq", [P, 2 * HEADS])
        ny = sb("ny", [P, 2 * HEADS])
        nt = sb("nt", [P, 2 * HEADS])
        inv = sb("inv", [P, SEQS, 2 * HEADS])
        qT = sb("qT", [P, 4, TOK])
        kT = sb("kT", [P, 4, TOK])
        scale = sb("scale", [P, 2, 4])
        mx = sb("mx", [P, 2, 4])
        shift = sb("shift", [P, 2, 4])
        prob = sb("prob", [P, HEADS, TOK])
        total = sb("total", [P, HEADS])
        tinv = sb("tinv", [P, HEADS])
        pT = sb("pT", [P, HEADS, TOK])
        oT = sb("oT", [P, 4, TOK])
        QK, PV, PS, PT, PO = 0, 2, 3, 5, 7
        norm_n = 2 + 3 * NEWTON
        block = ctx.enter_context(nc.Block())

        def steps(eng, step):
            for i in range(-2, 2):
                step(i, True, i >= -1, i >= 0, i >= 1)
            with eng.Fori(2, SEQS - 3) as i:
                step(i, True, True, True, True)
            for i in range(SEQS - 3, SEQS + 1):
                step(i, i < SEQS - 2, i < SEQS - 1, i < SEQS, True)

        @block.tensor
        def _(pe):
            def step(i, front, middle, current, back):
                if back:
                    pe.wait_ge(prob_ok, i)
                    if not isinstance(i, int) or i < SEQS:
                        pe.wait_ge(q_sb, i + 1)
                    for h in range(HEADS):
                        mm = pe.transpose(m.bank[:, PT + h // 4, (h % 4) * P:(h % 4 + 1) * P], prob[:, h, :],
                                          m.ident[:, :])
                    mm.then_inc(probT_mm, 1)
                if front:
                    pe.wait_ge(front_staged, i + 3)
                    at_least(pe, square_sb, i + 2)
                    at_least(pe, rope_k, i + 2)
                    for k in range(2):
                        mm = pe.matmul(m.bank[:, QK + k, :], hf[:, :],
                                       m.wqkv[:, layer, k * INNER:(k + 1) * INNER], start=True, stop=True)
                    mm.then_inc(qk_mm, 1)
                if back:
                    pe.wait_ge(v_sb, i)
                    pe.wait_ge(probTa_sb, i)
                    pe.wait_ge(probTb_sb, i)
                    at_least(pe, res_ok, i - 1)
                    for c in range(4):
                        for r in range(2):
                            h = 2 * c + r
                            mm = pe.matmul(m.bank[r * HD:(r + 1) * HD, PO, c * P:(c + 1) * P],
                                           v[:, h * HD:(h + 1) * HD], pT[:, 4 * r + c, :], start=True, stop=True)
                    mm.then_inc(out_mm, 1)
                if current:
                    pe.wait_ge(value_staged, i + 1)
                    pe.matmul(m.bank[:, PV, :], hv[:, :], m.wqkv[:, layer, 2 * INNER:], start=True, stop=True)\
                        .then_inc(v_mm, 1)
                if middle:
                    pe.wait_ge(rotated, i + 2)
                    for k in range(2):
                        for c in range(4):
                            mm = pe.transpose(m.bank[:, PT + k, c * P:(c + 1) * P],
                                              rot[:, k * HEADS + 2 * c:k * HEADS + 2 * c + 2, :]
                                              .rearrange("p h d -> p (h d)"), m.ident[:, :])
                    mm.then_inc(turn_mm, 1)
                if back:
                    pe.wait_ge(out_sb, i)
                    for c in range(4):
                        mm = pe.matmul(m.bank[:, PO, 0:TOK], m.wo[:, layer, c, :], oT[:, c, :],
                                       start=(c == 0), stop=(c == 3))
                    mm.then_inc(y_mm, 1)
                if middle:
                    at_least(pe, prob_sb, i + 1)
                    for r in range(2):
                        pe.matmul(m.bank[:, PS + r, :], m.ident16[:, :],
                                  m.mask16[:, :, :].rearrange("p h t -> p (h t)"), start=True, stop=False,
                                  skip_group_check=True)
                    pe.wait_ge(k_sb, i + 2)
                    pe.wait_ge(q_sb, i + 2)
                    for c in range(4):
                        for r in range(2):
                            rows = slice(r * HD, (r + 1) * HD)
                            mm = pe.matmul(m.bank[:, PS + r, c * P:(c + 1) * P], qT[rows, c, :], kT[rows, c, :],
                                           start=False, stop=(c == 3), skip_group_check=True)
                    mm.then_inc(score_mm, 1)
            steps(pe, step)

        @block.scalar
        def _(act):
            def exps(heads):
                for h in heads:
                    last = act.activation(prob[:, h, :], m.bank[:, PS + h // 4, (h % 4) * P:(h % 4 + 1) * P],
                                          ACT.Exp, bias=shift[:, h // 4, h % 4:h % 4 + 1],
                                          scale=scale[:, h // 4, h % 4:h % 4 + 1], accum_out=total[:, h:h + 1])
                return last

            def step(i, front, middle, current, back):
                if back:
                    act.wait_ge(probT_mm, i)
                    at_least(act, out_mm, i - 1)
                    act.copy(pT[:, 0:4, :].rearrange("p h t -> p (h t)"), m.bank[:, PT, :]).then_inc(probTa_sb, 1)
                if current:
                    act.wait_ge(shift_ready, i + 1)
                    at_least(act, inv_ready, i)
                    exps(range(2))
                if front:
                    act.wait_ge(qk_mm, i + 3)
                    at_least(act, norm_steps, (i + 1) * norm_n + 1)
                    act.activation(sq[:, :, :].rearrange("p h d -> p (h d)"),
                                   m.bank[:, QK:QK + 2, :].rearrange("p k n -> p (k n)"), ACT.Square)\
                        .then_inc(square_sb, 1)
                if current:
                    exps(range(2, HEADS)).then_inc(prob_sb, 1)
                    act.wait_ge(v_mm, i + 1)
                    at_least(act, out_mm, i)
                    act.copy(v[:, :], m.bank[:, PV, :]).then_inc(v_sb, 1)
                if middle:
                    act.wait_ge(turn_mm, i + 2)
                    at_least(act, score_mm, i + 1)
                    act.copy(kT[:, :, :].rearrange("p c t -> p (c t)"), m.bank[:, PT + 1, :]).then_inc(k_sb, 1)
                    act.copy(qT[:, :, :].rearrange("p c t -> p (c t)"), m.bank[:, PT, :]).then_inc(q_sb, 1)
            steps(act, step)

        @block.gpsimd
        def _(pool):
            def step(i, front, middle, current, back):
                if current:
                    pool.wait_ge(inv_ready, i + 1)
                    pool.tensor_tensor(prob[:, :, :], prob[:, :, :],
                                       tinv[:, :].unsqueeze(2).broadcast_to([P, HEADS, TOK]), ALU.mult)\
                        .then_inc(prob_ok, 1)
                if front:
                    pool.wait_ge(rope_k, i + 3)
                    at_least(pool, turn_mm, i + 2)
                    for k in range(2):
                        pool.tensor_tensor(rot[:, :, k * 32:k * 32 + 32], ta[:, :, k * 32:k * 32 + 32],
                                           tb[:, :, 32 - k * 32:64 - k * 32], ALU.add).then_inc(pool_steps, 1)
                    pool.wait_ge(norm_ready, i + 3)
                    pool.wait_ge(pool_steps, 2 * i + 6)
                    pool.tensor_tensor(rot[:, HEADS:, :], rot[:, HEADS:, :],
                                       inv[:, bass.ds(i + 2, 1), HEADS:].rearrange("p o h -> p (o h)")
                                       .unsqueeze(2).broadcast_to([P, HEADS, HD]), ALU.mult).then_inc(rotated, 1)
            steps(pool, step)

        @block.vector
        def _(dve):
            vec = nc.vector

            def stage(dst, s, staged):
                vec.tensor_copy(dst[:, :], m.res[:, bass.ds(s, 1), 0:TOK].rearrange("p o t -> p (o t)"))\
                    .then_inc(staged, 1)

            def rotate(k):
                heads = slice(k * HEADS, (k + 1) * HEADS)
                for n, t in enumerate((ta, tb)):
                    last = vec.tensor_tensor(t[:, heads, :],
                                             m.bank[:, QK + k, :].rearrange("p (h d) -> p h d", d=HD),
                                             m.tab[:, layer, n, k:k + 1, :].broadcast_to([P, HEADS, HD]), ALU.mult)
                return last

            def norm(s, k):
                if k > 0:
                    dve.wait_ge(norm_steps, s * norm_n + k)
                x, y, t = ssq[:, :], ny[:, :], nt[:, :]
                if k == 0:
                    made = vec.tensor_reduce(x, sq[:, :, :], AX.X, ALU.add)
                elif k == 1:
                    made = vec.tensor_scalar(x, x, 1e-24, None, ALU.max)
                elif k == 2:
                    made = vec.tensor_scalar(y.bitcast(I32), x.bitcast(I32), -0.5, RSQRT_MAGIC, ALU.mult, ALU.add)
                elif k % 3 == 0:
                    made = vec.tensor_tensor(t, y, y, ALU.mult)
                elif k % 3 == 1:
                    made = vec.scalar_tensor_tensor(out=t, in0=t, scalar=-0.5, in1=x, op0=ALU.mult, op1=ALU.mult)
                elif k < norm_n:
                    made = vec.scalar_tensor_tensor(out=y, in0=t, scalar=1.5, in1=y, op0=ALU.add, op1=ALU.mult)
                else:
                    made = vec.scalar_tensor_tensor(
                        out=inv[:, bass.ds(s, 1), :].rearrange("p o h -> p (o h)"), in0=t, scalar=1.5, in1=y,
                        op0=ALU.add, op1=ALU.mult)
                made.then_inc(norm_ready if k == norm_n else norm_steps, 1)

            stage(hf, 0, front_staged)

            def step(i, front, middle, current, back):
                if current:
                    dve.wait_ge(score_mm, i + 1)
                    at_least(dve, prob_sb, i)
                    vec.tensor_reduce(mx[:, :, :], m.bank[:, PS:PS + 2, :]
                                      .rearrange("p r (c t) -> p r c t", c=4), AX.X, ALU.max)\
                        .then_inc(max_steps, 1)
                if middle:
                    norm(i + 1, 7)
                if current:
                    vec.tensor_scalar(scale[:, :, :], inv[:, bass.ds(i, 1), 0:HEADS]
                                      .rearrange("p o (c r) -> p (o r) c", r=2), QK_SCALE, None, ALU.mult)\
                        .then_inc(max_steps, 1)
                if middle:
                    norm(i + 1, 8)
                if current:
                    dve.wait_ge(max_steps, 2 * i + 2)
                    vec.scalar_tensor_tensor(out=shift[:, :, :], in0=mx[:, :, :], scalar=-1.0, in1=scale[:, :, :],
                                             op0=ALU.mult, op1=ALU.mult).then_inc(shift_ready, 1)
                if middle:
                    norm(i + 1, 9)
                if back:
                    dve.wait_ge(probT_mm, i)
                    at_least(dve, out_mm, i - 1)
                    vec.tensor_copy(pT[:, 4:8, :].rearrange("p h t -> p (h t)"), m.bank[:, PT + 1, :])\
                        .then_inc(probTb_sb, 1)
                if middle:
                    norm(i + 1, 10)
                if current:
                    at_least(dve, v_mm, i)
                    stage(hv, i, value_staged)
                if middle:
                    norm(i + 1, 11)
                if front:
                    dve.wait_ge(qk_mm, i + 3)
                    if not isinstance(i, int) or i + 3 < SEQS:
                        stage(hf, i + 3, front_staged)
                    dve.wait_ge(square_sb, i + 3)
                    at_least(dve, pool_steps, 2 * i + 4)
                    rotate(0)
                if back:
                    dve.wait_ge(out_mm, i)
                    at_least(dve, y_mm, i - 1)
                    vec.tensor_copy(oT[:, :, :].rearrange("p c t -> p (c t)"), m.bank[:, PO, :]).then_inc(out_sb, 1)
                if front:
                    rotate(1).then_inc(rope_k, 1)
                    norm(i + 2, 0)
                if current:
                    dve.wait_ge(prob_sb, i + 1)
                    at_least(dve, prob_ok, i)
                    vec.reciprocal(tinv[:, :], total[:, :]).then_inc(inv_ready, 1)
                if front:
                    for k in range(1, 5):
                        norm(i + 2, k)
                if back:
                    dve.wait_ge(y_mm, i)
                for k in range(2):
                    if back:
                        rows = slice(k * HALF, (k + 1) * HALF)
                        r = m.res[rows, bass.ds(i - 1, 1), k:k + TOK].rearrange("p o t -> p (o t)")
                        last = vec.tensor_tensor(r, m.bank[rows, PO, 0:TOK], r, ALU.add)
                    if front:
                        norm(i + 2, 5 + k)
                if back:
                    last.then_inc(res_ok, 1)
            steps(dve, step)


def gated_ffn(nc, m, layer):
    with ExitStack() as ctx:
        sem = lambda name: ctx.enter_context(nc.semaphore(f"{name}{layer}"))
        sb = lambda name, shape: ctx.enter_context(nc.sbuf_tensor(f"{name}{layer}", shape, F32))
        staged, rows_mm, rows_sb, turn_mm, turn_sb, up_mm, gelu_sb, gate_sb, down_mm, res_ok, steps_sem = (
            sem(s) for s in ("f_staged", "f_rows_mm", "f_rows_sb", "f_turn_mm", "f_turn_sb", "f_up_mm",
                             "f_gelu_sb", "f_gate_sb", "f_down_mm", "f_res_ok", "f_steps"))
        hs = sb("f_hs", [P, GSEQ, TOK])
        hn = sb("f_hn", [P, GSEQ, DIM])
        hT = sb("f_hT", [P, GTOK])
        gelu = sb("f_gelu", [CH, 2, GTOK])
        u = sb("f_u", [CH, NCH, GTOK])
        stats = sb("f_stats", [P, GSEQ, 6])
        mv = sb("f_mv", [P, GSEQ, 2])
        ve = sb("f_ve", [P, GSEQ])
        rstd = sb("f_rstd", [P, GSEQ])
        tmp = sb("f_tmp", [P, GSEQ])
        PR, PT, PU, PD = 0, 1, 2, 6
        block = ctx.enter_context(nc.Block())

        def steps(eng, step):
            step(-1, True, False)
            step(0, True, True)
            with eng.Fori(1, GROUPS - 1) as g:
                step(g, True, True)
            step(GROUPS - 1, False, True)

        @block.tensor
        def _(pe):
            def step(g, norm, products):
                if norm:
                    pe.wait_ge(staged, g + 2)
                    at_least(pe, rows_sb, g + 1)
                    for j in range(GSEQ):
                        mm = pe.transpose(m.bank[:, PR, j * P:(j + 1) * P], hs[:, j, :], m.ident[:, :])
                    mm.then_inc(rows_mm, 1)
                if products:
                    pe.wait_ge(turn_sb, g + 1)
                    for c, (at, n) in enumerate(CHUNKS):
                        at_least(pe, gate_sb, NCH * g + c - 1)
                        for half in range(2):
                            mm = pe.matmul(m.bank[0:n, PU + 2 * (c % 2) + half, :],
                                           m.w1[:, layer, half * HID + at:half * HID + at + n], hT[:, :],
                                           start=True, stop=True)
                        mm.then_inc(up_mm, 1)
                if norm:
                    pe.wait_ge(rows_sb, g + 2)
                    at_least(pe, turn_sb, g + 1)
                    for j in range(GSEQ):
                        mm = pe.transpose(m.bank[:, PT, j * P:(j + 1) * P], hn[:, j, :], m.ident[:, :])
                    mm.then_inc(turn_mm, 1)
                if products:
                    at_least(pe, res_ok, g)
                    for c, (at, n) in enumerate(CHUNKS):
                        pe.wait_ge(gate_sb, NCH * g + c + 1)
                        mm = pe.matmul(m.bank[:, PD, :], m.w2[0:n, layer, c, :], u[0:n, c, :],
                                       start=(c == 0), stop=(c == NCH - 1))
                    mm.then_inc(down_mm, 1)
            steps(pe, step)

        @block.scalar
        def _(act):
            def step(g, norm, products):
                if products:
                    for c, (_, n) in enumerate(CHUNKS):
                        act.wait_ge(up_mm, NCH * g + c + 1)
                        at_least(act, gate_sb, NCH * g + c - 1)
                        act.activation(gelu[0:n, c % 2, :], m.bank[0:n, PU + 2 * (c % 2) + 1, :], ACT.Gelu,
                                       bias=m.b1eff[0:n, layer, NCH + c:NCH + c + 1]).then_inc(gelu_sb, 1)
                if norm:
                    act.wait_ge(turn_mm, g + 2)
                    at_least(act, up_mm, NCH * (g + 1))
                    act.copy(hT[:, :], m.bank[:, PT, :]).then_inc(turn_sb, 1)
            steps(act, step)

        @block.vector
        def _(dve):
            vec = nc.vector

            def step(g, norm, products):
                if norm:
                    at_least(dve, rows_mm, g + 1)
                    vec.tensor_copy(hs[:, :, :], m.res[:, bass.ds((g + 1) * GSEQ, GSEQ), 0:TOK]).then_inc(staged, 1)
                    dve.wait_ge(rows_mm, g + 2)
                    chain = Chain(dve, steps_sem, (g + 1) * LN_STEPS)
                    rows = m.bank[:, PR, :].rearrange("p (s d) -> p s d", s=GSEQ)
                    layernorm_stats(vec, chain, rows, stats, mv, ve, rstd, tmp, DIM)
                    at_least(dve, turn_mm, g + 1)
                    for j in range(GSEQ):
                        last = vec.tensor_scalar(hn[:, j, :], rows[:, j, :], mv[:, j, 0:1], rstd[:, j:j + 1],
                                                 ALU.subtract, ALU.mult)
                    last.then_inc(rows_sb, 1)
                if products:
                    for c, (_, n) in enumerate(CHUNKS):
                        dve.wait_ge(gelu_sb, NCH * g + c + 1)
                        at_least(dve, down_mm, g)
                        vec.scalar_tensor_tensor(out=u[0:n, c, :], in0=m.bank[0:n, PU + 2 * (c % 2), :],
                                                 scalar=m.b1eff[0:n, layer, c:c + 1], in1=gelu[0:n, c % 2, :],
                                                 op0=ALU.add, op1=ALU.mult).then_inc(gate_sb, 1)
                    dve.wait_ge(down_mm, g + 1)
                    for k in range(2):
                        rows = slice(k * HALF, (k + 1) * HALF)
                        r = m.res[rows, bass.ds(g * GSEQ, GSEQ), k:k + TOK]
                        last = vec.scalar_tensor_tensor(
                            out=r, in0=m.bank[rows, PD, :].rearrange("p (s t) -> p s t", s=GSEQ),
                            scalar=m.cols[rows, 2, layer:layer + 1], in1=r, op0=ALU.add, op1=ALU.add)
                    last.then_inc(res_ok, 1)
            steps(dve, step)


def ternary_mlp(nc, m, a, out):
    with ExitStack() as ctx:
        sem = lambda name: ctx.enter_context(nc.semaphore(name))
        sb = lambda name, shape: ctx.enter_context(nc.sbuf_tensor(name, shape, F32))
        w_loaded, x1_ok, cond_mm, cond_sb, fc_mm, gelu_sb, norm_ok, turn_mm, turn_sb = (
            sem(s) for s in ("l_w_loaded", "l_x1_ok", "l_cond_mm", "l_cond_sb", "l_fc_mm", "l_gelu_sb",
                             "l_norm_ok", "l_turn_mm", "l_turn_sb"))
        proj_mm, sum_ok, back_mm, back_sb, stored, steps_sem = (
            sem(s) for s in ("l_proj_mm", "l_sum_ok", "l_back_mm", "l_back_sb", "l_stored", "l_steps"))
        cT = sb("l_cT", [P, GSEQ, TOK])
        gl = sb("l_gl", [P, GSEQ, FC])
        gT = sb("l_gT", [P, FC // P, GTOK])
        oT = sb("l_oT", [P, GTOK])
        o = sb("l_o", [P, 2, GTOK])
        stats = sb("l_stats", [P, GSEQ, 6])
        mv = sb("l_mv", [P, GSEQ, 2])
        ve = sb("l_ve", [P, GSEQ])
        rstd = sb("l_rstd", [P, GSEQ])
        tmp = sb("l_tmp", [P, GSEQ])
        PC, PF, PT, PP, PB = 0, 1, 3, 5, 6
        block = ctx.enter_context(nc.Block())

        @block.sync
        def _(sp):
            def load(g):
                for j in range(GSEQ):
                    subject = sp.value_load(m.idx[0:1, 1, GSEQ * g + j:GSEQ * g + j + 1], min_val=0, max_val=15)
                    sp.dma_start(m.cwc[:, j:j + 1, :],
                                 a["cwc"][bass.ds(subject, 1), :, :].rearrange("o p n -> p o n"))\
                        .then_inc(w_loaded, 16)

            load(0)
            for g in range(GROUPS):
                if g + 1 < GROUPS:
                    sp.wait_ge(cond_mm, g + 1)
                    load(g + 1)
                sp.wait_ge(back_sb, g + 1)
                sp.dma_start(out[GSEQ * g:GSEQ * (g + 1), :, :].rearrange("s t d -> t s d"),
                             o[:, g % 2, :].rearrange("p (s d) -> p s d", s=GSEQ)).then_inc(stored, 16)
            sp.wait_ge(stored, 16 * GROUPS)

        @block.tensor
        def _(pe):
            def up(g):
                pe.wait_ge(x1_ok, g + 1)
                pe.wait_ge(w_loaded, 16 * GSEQ * (g + 1))
                at_least(pe, cond_sb, g)
                for j in range(GSEQ):
                    mm = pe.matmul(m.bank[:, PC, j * P:(j + 1) * P], m.cwc[:, j, :], m.x1T[:, GSEQ * g + j, :],
                                   start=True, stop=True)
                mm.then_inc(cond_mm, 1)

            def fc(g):
                pe.wait_ge(cond_sb, g + 1)
                for j in range(GSEQ):
                    at_least(pe, gelu_sb, GSEQ * g + j - 1)
                    pe.matmul(m.bank[:, PF + j % 2, :], cT[:, j, :], m.wfT[:, :], start=True, stop=True)\
                        .then_inc(fc_mm, 1)

            def turn(g):
                pe.wait_ge(norm_ok, g + 1)
                for c in range(FC // P):
                    at_least(pe, turn_sb, 4 * g + c - 1)
                    for j in range(GSEQ):
                        mm = pe.transpose(m.bank[:, PT + c % 2, j * P:(j + 1) * P], gl[:, j, c * P:(c + 1) * P],
                                          m.ident[:, :])
                    mm.then_inc(turn_mm, 1)

            def down(g):
                at_least(pe, sum_ok, g)
                for c in range(FC // P):
                    pe.wait_ge(turn_sb, 4 * g + c + 1)
                    mm = pe.matmul(m.bank[:, PP, :], m.wpT[:, c, :], gT[:, c, :], start=(c == 0), stop=(c == 3))
                mm.then_inc(proj_mm, 1)

            def store(g):
                pe.wait_ge(sum_ok, g + 1)
                at_least(pe, back_sb, g)
                for j in range(GSEQ):
                    mm = pe.transpose(m.bank[:, PB, j * P:(j + 1) * P], oT[:, j * P:(j + 1) * P], m.ident[:, :])
                mm.then_inc(back_mm, 1)

            up(0)
            fc(0)
            for g in range(GROUPS):
                if g + 1 < GROUPS:
                    up(g + 1)
                turn(g)
                down(g)
                if g + 1 < GROUPS:
                    fc(g + 1)
                store(g)

        @block.scalar
        def _(act):
            def gelu(g):
                at_least(act, turn_mm, 4 * g)
                for j in range(GSEQ):
                    act.wait_ge(fc_mm, GSEQ * g + j + 1)
                    act.activation(gl[:, j, :], m.bank[:, PF + j % 2, :], ACT.Gelu).then_inc(gelu_sb, 1)

            def scaled(g):
                for c in range(FC // P):
                    act.wait_ge(turn_mm, 4 * g + c + 1)
                    if c == 0:
                        at_least(act, proj_mm, g)
                    act.activation(gT[:, c, :], m.bank[:, PT + c % 2, :], ACT.Identity,
                                   scale=m.ln1[:, 0, c:c + 1], bias=m.ln1[:, 1, c:c + 1]).then_inc(turn_sb, 1)

            gelu(0)
            for g in range(GROUPS):
                scaled(g)
                if g + 1 < GROUPS:
                    gelu(g + 1)
                act.wait_ge(back_mm, g + 1)
                at_least(act, stored, 16 * (g - 1))
                act.copy(o[:, g % 2, :], m.bank[:, PB, :]).then_inc(back_sb, 1)

        @block.vector
        def _(dve):
            vec = nc.vector

            def x1(g):
                for k in range(2):
                    rows = slice(k * HALF, (k + 1) * HALF)
                    s = slice(GSEQ * g, GSEQ * (g + 1))
                    last = vec.tensor_tensor(m.x1T[rows, s, :], m.res[rows, s, k:k + TOK], m.xT[rows, s, :], ALU.add)
                last.then_inc(x1_ok, 1)

            def bias(g):
                dve.wait_ge(cond_mm, g + 1)
                at_least(dve, fc_mm, GSEQ * g)
                vec.tensor_tensor(cT[:, :, :], m.bank[:, PC, :].rearrange("p (s t) -> p s t", s=GSEQ),
                                  m.bcT[:, GSEQ * g:GSEQ * (g + 1)].unsqueeze(2).broadcast_to([P, GSEQ, TOK]),
                                  ALU.add).then_inc(cond_sb, 1)

            def norm(g):
                dve.wait_ge(gelu_sb, GSEQ * (g + 1))
                chain = Chain(dve, steps_sem, g * LN_STEPS)
                layernorm_stats(vec, chain, gl, stats, mv, ve, rstd, tmp, FC)
                for j in range(GSEQ):
                    last = vec.tensor_scalar(gl[:, j, :], gl[:, j, :], mv[:, j, 0:1], rstd[:, j:j + 1],
                                             ALU.subtract, ALU.mult)
                last.then_inc(norm_ok, 1)

            x1(0)
            bias(0)
            x1(1)
            norm(0)
            for g in range(GROUPS):
                if g + 1 < GROUPS:
                    bias(g + 1)
                if g + 2 < GROUPS:
                    x1(g + 2)
                dve.wait_ge(proj_mm, g + 1)
                at_least(dve, back_mm, g)
                vec.tensor_tensor(oT[:, :], m.bank[:, PP, :],
                                  m.x1T[:, GSEQ * g:GSEQ * (g + 1), :].rearrange("p s t -> p (s t)"), ALU.add)\
                    .then_inc(sum_ok, 1)
                if g + 1 < GROUPS:
                    norm(g + 1)


def program(nc, a, out):
    with ExitStack() as ctx:
        m = Memory(nc, ctx)
        prepare(nc, m, a)
        conditioned_adapter(nc, m, a)
        for layer in range(DEPTH):
            attention(nc, m, layer)
            gated_ffn(nc, m, layer)
        ternary_mlp(nc, m, a, out)


def shape_constants():
    i, j = np.arange(TOK)[:, None], np.arange(TOK)[None, :]
    masked = (i < j) | (i > j + WINDOW)
    mask = np.where(masked, -1e30, 0.0).astype(np.float32)
    half = np.arange(0, HD, 2, dtype=np.float32)
    inv_freq = (1.0 / np.float32(10000.0) ** (half / HD)).astype(np.float32)
    t = np.arange(TOK, dtype=np.float32)
    freqs = (t[:, None] * inv_freq[None, :]).astype(np.float32)
    base = ((half + 0.4 * HD) / (1.4 * HD)).astype(np.float32)
    power = ((t - TOK // 2) / float(WINDOW // 2)).astype(np.float32)
    xpos = (base[None, :] ** power[:, None]).astype(np.float32)
    two = lambda z: np.concatenate([z, z], axis=-1)
    cos, sin, xpos = two(np.cos(freqs)), two(np.sin(freqs)), two(xpos)
    sin = sin * np.where(np.arange(HD) < HD // 2, 1.0, -1.0)
    rope = np.stack([np.stack([cos * xpos, cos / xpos], 1), np.stack([sin * xpos, sin / xpos], 1)], 1)
    return {
        "ident": np.eye(P, dtype=np.float32),
        "mask": mask,
        "rope": rope.astype(np.float32),
        "part": np.arange(16, dtype=np.float32)[:, None],
    }


def kernel(**inputs):
    import concourse.bacc as bacc
    from concourse.bass_utils import run_bass_kernel_spmd

    x = {k: np.asarray(v) for k, v in inputs.items()}
    arrays = {
        "x": x["x"], "id8": x["itok_B_0_8"], "id15": x["itok_B_0_15"],
        "rows8": np.concatenate([x["L0_cond_b1"], x["L0_cond_gamma"], x["L0_cond_beta"]], axis=1),
        "rows15": x["L1_cond_b"],
        "cw1": x["L0_cond_W1"],
        "cw2": np.concatenate([x["L0_cond_W2"], x["L0_cond_b2"][:, None, :]], axis=1),
        "cwc": x["L1_cond_weights"],
        "wqkv": x["L0_ffn_wqkv"], "wo": x["L0_ffn_wo"], "w1": x["L0_ffn_w1"], "w2": x["L0_ffn_w2"],
        "b1": x["L0_ffn_b1"], "b2": x["L0_ffn_b2"], "ln_g0": x["L0_ffn_ln_g"], "ln_b0": x["L0_ffn_ln_b"],
        "qks": np.stack([x["L0_ffn_q_scale"], x["L0_ffn_k_scale"]], axis=1).reshape(-1),
        "W_fc": x["L1_ffn_W_fc"], "W_proj": x["L1_ffn_W_proj"], "ln_w": x["L1_ffn_ln_w"], "ln_b": x["L1_ffn_ln_b"],
    }
    arrays |= shape_constants()
    nc = bacc.Bacc("TRN2", target_bir_lowering=False, num_devices=1)
    feed, aps = {}, {}
    for name, value in arrays.items():
        value = np.ascontiguousarray(value)
        feed[f"in_{name}"] = value
        aps[name] = nc.dram_tensor(f"in_{name}", value.shape, mybir.dt.from_np(value.dtype),
                                   kind="ExternalInput").ap()
    out = nc.dram_tensor("out_0", (SEQS, TOK, DIM), F32, kind="ExternalOutput").ap()
    program(nc, aps, out)
    return run_bass_kernel_spmd(nc, [feed], core_ids=[0]).results[0]["out_0"]
```

```python
from contextlib import ExitStack

import numpy as np

import concourse.bass as bass
from concourse import mybir

F32 = mybir.dt.float32
BF16 = mybir.dt.bfloat16
I32 = mybir.dt.int32
F32R = mybir.dt.float32r
ACT = mybir.ActivationFunctionType
ALU = mybir.AluOpType
AX = mybir.AxisListType

P = 128
SEQS, TOK, DIM = 16, 128, 128
HALF = DIM // 2
HEADS, HD = 8, 64
INNER = HEADS * HD
DEPTH = 2
HID = int(DIM * 4 * 2 / 3)
NCH = 3
CH = -(-HID // NCH)
CHUNKS = [(c * CH, min(CH, HID - c * CH)) for c in range(NCH)]
ADIM = 32
FC = 512
W2_AT, GAMMA_AT, BETA_AT, B1_AT, COND = ADIM, ADIM + DIM, ADIM + DIM + 1, ADIM + DIM + 2, ADIM + DIM + 3
GSEQ = 4
GROUPS = SEQS // GSEQ
GTOK = GSEQ * TOK
SKEW = 130
WINDOW = 64
QK_SCALE = 8.0
LN_EPS = 1e-5
RSQRT_MAGIC = float(0x5F3759DF)
NEWTON = 3
RSQRT_OPS = 1 + 3 * NEWTON


class Chain:

    def __init__(self, eng, sem, base):
        self.eng, self.sem, self.base, self.n = eng, sem, base, 0

    def add(self, instruction):
        instruction.then_inc(self.sem, 1)
        self.n += 1

    def wait(self):
        self.eng.wait_ge(self.sem, self.base + self.n)


def rsqrt(vec, chain, x, y, t):
    chain.add(vec.tensor_scalar(y.bitcast(I32), x.bitcast(I32), -0.5, RSQRT_MAGIC, ALU.mult, ALU.add))
    for _ in range(NEWTON):
        chain.wait()
        chain.add(vec.tensor_tensor(t, y, y, ALU.mult))
        chain.wait()
        chain.add(vec.scalar_tensor_tensor(out=t, in0=t, scalar=-0.5, in1=x, op0=ALU.mult, op1=ALU.mult))
        chain.wait()
        chain.add(vec.scalar_tensor_tensor(out=y, in0=t, scalar=1.5, in1=y, op0=ALU.add, op1=ALU.mult))
    chain.wait()


def product(pe, out, left, right):
    (lh, ll), (rh, rl) = left, right
    pe.matmul(out, lh, rh, start=True, stop=False)
    pe.matmul(out, lh, rl, start=False, stop=False)
    return pe.matmul(out, ll, rh, start=False, stop=True)


def at_least(eng, sem, value):
    if not isinstance(value, int) or value > 0:
        eng.wait_ge(sem, value)


class Memory:

    def __init__(self, nc, ctx):
        def sb(name, shape, dt=F32):
            return ctx.enter_context(nc.sbuf_tensor(name, shape, dt))

        self.bank = ctx.enter_context(nc.psum_tensor("bank", [P, 8, 512], F32))
        self.ident = sb("ident", [P, P])
        self.ident16 = sb("ident16", [P, P], BF16)
        self.mask16 = sb("mask16", [P, 4, TOK], BF16)
        self.mask = sb("mask", [P, TOK])
        self.rope = sb("rope", [P, 2, 2, HD])
        self.ones = sb("ones", [P, P])
        self.x_in = sb("x_in", [P, SEQS, DIM])
        self.xT = sb("xT", [P, SEQS, TOK])
        self.res = sb("res", [P, SEQS, SKEW])
        self.x1T = sb("x1T", [P, SEQS, TOK])
        self.idx = sb("idx", [1, 2, SEQS], I32)
        self.cond = sb("cond", [P, SEQS, COND])
        self.cwc = sb("cwc", [P, SEQS, DIM + 1])
        self.wqkv = sb("wqkv", [P, DEPTH, 3 * INNER])
        self.wqkv2 = [sb(f"wqkv_{k}", [P, DEPTH, 3 * INNER], F32R) for k in ("hi", "lo")]
        self.wo = sb("wo", [P, DEPTH, INNER // P, DIM])
        self.w1 = sb("w1", [P, DEPTH, 2 * HID])
        self.w1s = [sb(f"w1_{k}", [P, DEPTH, 2 * HID], F32R) for k in ("hi", "lo")]
        self.w2 = sb("w2", [CH, DEPTH, NCH, DIM])
        self.b1 = sb("b1", [CH, DEPTH, 2 * NCH])
        self.b1eff = sb("b1eff", [CH, DEPTH, 2 * NCH])
        self.cols = sb("cols", [P, 3, DEPTH])
        self.qks = sb("qks", [P, DEPTH, 2, HD])
        self.tab = sb("tab", [P, DEPTH, 2, 2, HD])
        self.wf = sb("wf", [P, 2, FC])
        self.wneg = sb("wneg", [P, 2, FC])
        self.wfT = sb("wfT", [P, FC])
        self.wpT = sb("wpT", [P, FC // P, DIM])
        self.ln1 = sb("ln1", [P, 2, FC // P])
        self.absum = sb("absum", [P, 2])
        self.thr = sb("thr", [P, 2])


def prepare_and_adapt(nc, m, a):
    with ExitStack() as ctx:
        sem = lambda name: ctx.enter_context(nc.semaphore(name))
        sb = lambda name, shape: ctx.enter_context(nc.sbuf_tensor(name, shape, F32))
        idx_loaded, const_loaded, table_loaded, tern_loaded, qkv_loaded, w1_loaded, rest_loaded = (
            sem(s) for s in ("idx_loaded", "const_loaded", "table_loaded", "tern_loaded", "qkv_loaded",
                             "w1_loaded", "rest_loaded"))
        x_loaded = [sem(f"x_loaded{g}") for g in range(GROUPS)]
        cond_loaded = [[sem(f"cond_loaded{g}_{q}") for q in ("sp", "pool")] for g in range(GROUPS)]
        filled, one_row, sums, sum_all, ternary, turned, b1_mm, split, scaled, w1_hi, prep_steps = (
            sem(s) for s in ("filled", "one_row", "sums", "sum_all", "ternary", "turned", "b1_mm", "split", "scaled",
                             "w1_hi", "prep_steps"))
        xt_mm, xt_sb, h1_mm, h1_sb, ad_mm, sum_sb, xn_sb, xn_mm, res_sb, stat_steps = (
            sem(s) for s in ("xt_mm", "xt_sb", "h1_mm", "h1_sb", "ad_mm", "sum_sb", "xn_sb", "xn_mm", "res_sb",
                             "stat_steps"))
        h1 = sb("h1", [ADIM + 1, 2, GSEQ, TOK])
        xr = sb("xr", [P, SEQS, DIM])
        stats = sb("c_stats", [P, SEQS, 6])
        mv = sb("c_mv", [P, SEQS, 2])
        ve = sb("c_ve", [P, SEQS])
        rstd = sb("c_rstd", [P, SEQS])
        tmp = sb("c_tmp", [P, SEQS])
        PX, PH, PA, PN = 0, 2, 4, 6
        block = ctx.enter_context(nc.Block())

        def load_cond(eng, g, j):
            s = GSEQ * g + j
            lang = eng.value_load(m.idx[0:1, 0, s:s + 1], min_val=0, max_val=9)
            eng.dma_start(m.cond[:, s:s + 1, :], a["cond"][bass.ds(lang, 1), :, :].rearrange("o p n -> p o n"))\
                .then_inc(cond_loaded[g][j // 2], 16)

        def to_residual(scale_bias, g):
            for j in range(GSEQ):
                s = GSEQ * g + j
                for k in range(2):
                    rows = slice(k * HALF, (k + 1) * HALF)
                    last = scale_bias(m.res[rows, s, k:k + TOK], m.bank[rows, PN + g % 2, j * P:(j + 1) * P],
                                      m.cond[rows, s, GAMMA_AT:GAMMA_AT + 1], m.cond[rows, s, BETA_AT:BETA_AT + 1])
            return last

        @block.sync
        def _(sp):
            sp.dma_start(m.idx[:, :, :], a["idx"].rearrange("k (o s) -> o k s", o=1)).then_inc(idx_loaded, 16)
            sp.dma_start(m.ident[:, :], a["ident"]).then_inc(const_loaded, 16)
            sp.wait_ge(idx_loaded, 16)
            for g in range(GROUPS):
                for j in range(2):
                    load_cond(sp, g, j)
            sp.dma_start(m.wqkv[:, :, :], a["wqkv"].rearrange("l p n -> p l n")).then_inc(qkv_loaded, 16)
            for dst, name in ((m.mask[:, :], "mask"), (m.rope[:, :, :, :], "rope")):
                sp.dma_start(dst, a[name]).then_inc(table_loaded, 16)
            sp.dma_start(m.qks[:, :, :, :].rearrange("p l t d -> p (l t d)"),
                         a["qks"].partition_broadcast(P)).then_inc(table_loaded, 16)
            sp.dma_start(m.w1[:, :, :], a["w1"].rearrange("l p n -> p l n")).then_inc(w1_loaded, 16)
            for k, name in enumerate(("ln_g0", "ln_b0", "b2")):
                sp.dma_start(m.cols[:, k, :], a[name].rearrange("l p -> p l"),
                             allow_slow_non_contiguous=True).then_inc(w1_loaded, 16)
            for c, (at, n) in enumerate(CHUNKS):
                for half in range(2):
                    sp.dma_start(m.b1[0:n, :, half * NCH + c],
                                 a["b1"][:, half * HID + at:half * HID + at + n].rearrange("l p -> p l"),
                                 allow_slow_non_contiguous=True).then_inc(w1_loaded, 16)
            sp.dma_start(m.wo[:, :, :, :], a["wo"].rearrange("l (c p) n -> p l c n", p=P)).then_inc(rest_loaded, 16)
            for c, (at, n) in enumerate(CHUNKS):
                sp.dma_start(m.w2[0:n, :, c, :], a["w2"][:, at:at + n, :].rearrange("l p n -> p l n"))\
                    .then_inc(rest_loaded, 16)
            for k, name in enumerate(("ln_w", "ln_b")):
                sp.dma_start(m.ln1[:, k, :], a[name].rearrange("(c p) -> p c", p=P),
                             allow_slow_non_contiguous=True).then_inc(rest_loaded, 16)
            sp.wait_ge(rest_loaded, 16 * (3 + NCH))

        @block.gpsimd
        def _(pool):
            pool.memset(m.ones[:, :], 1.0).then_inc(filled, 1)
            pool.wait_ge(idx_loaded, 16)
            for g in range(GROUPS):
                for j in range(2, GSEQ):
                    load_cond(pool, g, j)
                if g == 0:
                    pool.wait_ge(filled, 1)
                    pool.memset(m.res[:, :, :], 0.0).then_inc(filled, 1)
            for layer in range(DEPTH):
                pool.wait_ge(split, layer + 1)
                pool.tensor_tensor(m.wqkv2[1][:, layer, :], m.wqkv[:, layer, :],
                                   m.wqkv2[0][:, layer, :].bitcast(F32), ALU.subtract)

        @block.tensor
        def _(pe):
            def turn_x(g):
                pe.wait_ge(x_loaded[g], 16)
                at_least(pe, xt_sb, g - 1)
                for j in range(GSEQ):
                    mm = pe.transpose(m.bank[:, PX + g % 2, j * P:(j + 1) * P], m.x_in[:, GSEQ * g + j, :],
                                      m.ident[:, :])
                mm.then_inc(xt_mm, 1)

            def down_project(g):
                pe.wait_ge(xt_sb, g + 1)
                for loaded in cond_loaded[g]:
                    pe.wait_ge(loaded, 16 * GSEQ // 2)
                at_least(pe, h1_sb, g - 1)
                for j in range(GSEQ):
                    mm = pe.matmul(m.bank[0:ADIM, PH + g % 2, j * P:(j + 1) * P], m.cond[:, GSEQ * g + j, 0:ADIM],
                                   m.xT[:, GSEQ * g + j, :], start=True, stop=True)
                mm.then_inc(h1_mm, 1)

            def up_project(g):
                pe.wait_ge(h1_sb, g + 1)
                at_least(pe, sum_sb, g - 1)
                for j in range(GSEQ):
                    mm = pe.matmul(m.bank[:, PA + g % 2, j * P:(j + 1) * P], h1[:, g % 2, j, :],
                                   m.cond[0:ADIM + 1, GSEQ * g + j, W2_AT:W2_AT + DIM], start=True, stop=True)
                mm.then_inc(ad_mm, 1)

            def turn_back(g):
                pe.wait_ge(xn_sb, g + 1)
                at_least(pe, res_sb, g - 1)
                for j in range(GSEQ):
                    mm = pe.transpose(m.bank[:, PN + g % 2, j * P:(j + 1) * P], xr[:, GSEQ * g + j, :],
                                      m.ident[:, :])
                mm.then_inc(xn_mm, 1)

            pe.wait_ge(const_loaded, 16)
            turn_x(0)
            turn_x(1)
            pe.wait_ge(filled, 1)
            pe.wait_ge(sums, 2)
            pe.matmul(m.bank[:, PN, 0:2], m.ones[:, :], m.absum[:, :], start=True, stop=True).then_inc(sum_all, 1)
            down_project(0)
            turn_x(2)
            down_project(1)
            pe.wait_ge(one_row, 1)
            up_project(0)
            turn_x(3)
            down_project(2)
            up_project(1)
            down_project(3)
            up_project(2)
            up_project(3)
            pe.wait_ge(ternary, 1)
            for k in range(2):
                for c in range(4):
                    mm = pe.transpose(m.bank[:, PX + k, c * P:(c + 1) * P], m.wf[:, k, c * P:(c + 1) * P],
                                      m.ident[:, :])
            mm.then_inc(turned, 1)
            turn_back(0)
            turn_back(1)
            pe.wait_ge(w1_loaded, 16 * (4 + 2 * NCH))
            for layer in range(DEPTH):
                for k in range(2 * NCH):
                    at, n = CHUNKS[k % NCH]
                    at += (k // NCH) * HID
                    mm = pe.matmul(m.bank[0:n, PH, layer * 2 * NCH + k:layer * 2 * NCH + k + 1],
                                   m.w1[:, layer, at:at + n], m.cols[:, 1, layer:layer + 1],
                                   start=True, stop=True)
            mm.then_inc(b1_mm, 1)
            turn_back(2)
            turn_back(3)

        @block.scalar
        def _(act):
            for g in range(GROUPS):
                act.dma_start(m.x_in[:, GSEQ * g:GSEQ * (g + 1), :],
                              a["x"][GSEQ * g:GSEQ * (g + 1), :, :].rearrange("s t d -> t s d"))\
                    .then_inc(x_loaded[g], 16)
            act.dma_start(m.wf[:, 0, :].rearrange("p (c n) -> p c n", c=4),
                          a["W_fc"].rearrange("(c p) n -> p c n", p=P)).then_inc(tern_loaded, 16)
            act.dma_start(m.wf[:, 1, :], a["W_proj"]).then_inc(tern_loaded, 16)

            def copy_x(g):
                act.wait_ge(xt_mm, g + 1)
                act.copy(m.xT[:, GSEQ * g:GSEQ * (g + 1), :].rearrange("p s t -> p (s t)"),
                         m.bank[:, PX + g % 2, :]).then_inc(xt_sb, 1)

            def relu(g):
                act.wait_ge(h1_mm, g + 1)
                at_least(act, ad_mm, g - 1)
                for j in range(GSEQ):
                    last = act.activation(h1[0:ADIM, g % 2, j, :], m.bank[0:ADIM, PH + g % 2, j * P:(j + 1) * P],
                                          ACT.Relu, bias=m.cond[0:ADIM, GSEQ * g + j, B1_AT:B1_AT + 1])
                last.then_inc(h1_sb, 1)

            def residual_of(g):
                act.wait_ge(xn_mm, g + 1)
                to_residual(lambda dst, src, gamma, beta: act.activation(dst, src, ACT.Identity, scale=gamma,
                                                                         bias=beta), g).then_inc(res_sb, 1)

            copy_x(0)
            copy_x(1)
            relu(0)
            copy_x(2)
            relu(1)
            copy_x(3)
            relu(2)
            relu(3)
            act.wait_ge(qkv_loaded, 16)
            for layer in range(DEPTH):
                act.copy(m.wqkv2[0][:, layer, :], m.wqkv[:, layer, :]).then_inc(split, 1)
            act.wait_ge(turned, 1)
            act.copy(m.wfT[:, :], m.bank[:, PX, :])
            act.copy(m.wpT[:, :, :].rearrange("p c n -> p (c n)"), m.bank[:, PX + 1, :])
            act.wait_ge(filled, 2)
            residual_of(0)
            act.wait_ge(res_sb, 2)
            residual_of(2)
            for layer in range(DEPTH):
                act.wait_ge(scaled, layer + 1)
                act.copy(m.w1s[0][:, layer, :], m.w1[:, layer, :]).then_inc(w1_hi, 1)

        @block.vector
        def _(dve):
            vec = nc.vector
            chain = Chain(dve, prep_steps, 0)
            vec.memset(h1[ADIM:ADIM + 1, :, :, :], 1.0).then_inc(one_row, 1)
            dve.wait_ge(tern_loaded, 16 * 2)
            for k in range(2):
                vec.tensor_reduce(m.absum[:, k:k + 1], m.wf[:, k, :], AX.X, ALU.add, apply_absolute_value=True)\
                    .then_inc(sums, 1)
            dve.wait_ge(sum_all, 1)
            chain.add(vec.tensor_scalar(m.thr[:, :], m.bank[:, PN, 0:2], 1.0 / (FC * DIM), 1e-6,
                                        ALU.mult, ALU.add))
            chain.wait()
            chain.add(vec.tensor_scalar(m.thr[:, :], m.thr[:, :], 0.5, None, ALU.mult))
            chain.wait()
            for k in range(2):
                chain.add(vec.tensor_scalar(m.wneg[:, k, :], m.wf[:, k, :], -1.0, m.thr[:, k:k + 1],
                                            ALU.mult, ALU.is_gt))
            chain.wait()
            for k in range(2):
                last = vec.scalar_tensor_tensor(out=m.wf[:, k, :], in0=m.wf[:, k, :], scalar=m.thr[:, k:k + 1],
                                                in1=m.wneg[:, k, :], op0=ALU.is_gt, op1=ALU.subtract)
            last.then_inc(ternary, 1)

            norm_chain = Chain(dve, stat_steps, 0)

            def add_adapter(g):
                dve.wait_ge(ad_mm, g + 1)
                s = slice(GSEQ * g, GSEQ * (g + 1))
                vec.tensor_tensor(xr[:, s, :].rearrange("p s t -> p (s t)"), m.bank[:, PA + g % 2, :],
                                  m.x_in[:, s, :].rearrange("p s t -> p (s t)"), ALU.add).then_inc(sum_sb, 1)
                dve.wait_ge(sum_sb, g + 1)
                row_stats(vec, norm_chain, xr[:, s, :], stats[:, s, :])

            def normalise(g):
                s = slice(GSEQ * g, GSEQ * (g + 2))
                inverse_deviation(vec, norm_chain, stats[:, s, :], mv[:, s, :], ve[:, s], rstd[:, s], tmp[:, s],
                                  DIM)
                for h in (g, g + 1):
                    for t in range(GSEQ * h, GSEQ * (h + 1)):
                        last = vec.tensor_scalar(xr[:, t, :], xr[:, t, :], mv[:, t, 0:1], rstd[:, t:t + 1],
                                                 ALU.subtract, ALU.mult)
                    last.then_inc(xn_sb, 1)

            def residual_of(g):
                dve.wait_ge(xn_mm, g + 1)
                dve.wait_ge(res_sb, g)
                to_residual(lambda dst, src, gamma, beta: vec.tensor_scalar(dst, src, gamma, beta,
                                                                            ALU.mult, ALU.add), g)\
                    .then_inc(res_sb, 1)

            add_adapter(0)
            add_adapter(1)
            normalise(0)
            add_adapter(2)
            add_adapter(3)
            normalise(2)
            dve.wait_ge(const_loaded, 16)
            dve.wait_ge(table_loaded, 16 * 3)
            vec.tensor_copy(m.ident16[:, :], m.ident[:, :])
            vec.tensor_copy(m.mask16[:, :, :], m.mask[:, :].unsqueeze(1).broadcast_to([P, 4, TOK]))
            for layer in range(DEPTH):
                for k in range(2):
                    vec.tensor_tensor(m.tab[:, layer, k, :, :], m.rope[:, k, :, :], m.qks[:, layer, :, :], ALU.mult)
            residual_of(1)
            dve.wait_ge(b1_mm, 1)
            for layer in range(DEPTH):
                vec.tensor_scalar(m.w1[:, layer, :], m.w1[:, layer, :], m.cols[:, 0, layer:layer + 1],
                                  None, ALU.mult).then_inc(scaled, 1)
                for k in range(2 * NCH):
                    n = CHUNKS[k % NCH][1]
                    vec.tensor_tensor(m.b1eff[0:n, layer, k:k + 1],
                                      m.bank[0:n, PH, layer * 2 * NCH + k:layer * 2 * NCH + k + 1],
                                      m.b1[0:n, layer, k:k + 1], ALU.add)
            residual_of(3)
            for layer in range(DEPTH):
                dve.wait_ge(w1_hi, layer + 1)
                vec.tensor_tensor(m.w1s[1][:, layer, :], m.w1[:, layer, :], m.w1s[0][:, layer, :].bitcast(F32),
                                  ALU.subtract)


def row_stats(vec, chain, rows, stats):
    for j in range(rows.shape[1]):
        chain.add(vec.bn_stats(stats[:, j, :], rows[:, j, :]))


def inverse_deviation(vec, chain, stats, mv, ve, rstd, tmp, width):
    chain.wait()
    (me, qe), (mo, qo) = ((stats[:, :, 3 * k + 1], stats[:, :, 3 * k + 2]) for k in range(2))
    mean = mv[:, :, 0]
    chain.add(vec.tensor_tensor(mean, me, mo, ALU.add))
    chain.add(vec.tensor_tensor(tmp, me, mo, ALU.subtract))
    chain.add(vec.tensor_tensor(ve, qe, qo, ALU.add))
    chain.wait()
    chain.add(vec.tensor_scalar(mean, mean, 0.5, None, ALU.mult))
    chain.add(vec.scalar_tensor_tensor(out=tmp, in0=tmp, scalar=0.25, in1=tmp, op0=ALU.mult, op1=ALU.mult))
    chain.add(vec.tensor_scalar(ve, ve, 1.0 / width, LN_EPS, ALU.mult, ALU.add))
    chain.wait()
    chain.add(vec.tensor_tensor(ve, ve, tmp, ALU.add))
    chain.wait()
    rsqrt(vec, chain, ve, rstd, tmp)


def layernorm_stats(vec, chain, rows, stats, mv, ve, rstd, tmp, width):
    row_stats(vec, chain, rows, stats)
    inverse_deviation(vec, chain, stats, mv, ve[:, :], rstd[:, :], tmp[:, :], width)


LN_STEPS = GSEQ + 7 + RSQRT_OPS


def attention(nc, m, a, layer):
    with ExitStack() as ctx:
        sem = lambda name: ctx.enter_context(nc.semaphore(f"{name}{layer}"))
        sb = lambda name, shape: ctx.enter_context(nc.sbuf_tensor(f"{name}{layer}", shape, F32))
        front_staged, value_staged, qk_mm, v_mm, v_sb = (
            sem(s) for s in ("front_staged", "value_staged", "qk_mm", "v_mm", "v_sb"))
        square_sb, rope_k, norm_ready, rotated, turn_mm, turned_sb = (
            sem(s) for s in ("square_sb", "rope_k", "norm_ready", "rotated", "turn_mm", "turned_sb"))
        score_mm, shift_ready, prob_sb, inv_ready, prob_ok, probT_mm, probT_sb = (
            sem(s) for s in ("score_mm", "shift_ready", "prob_sb", "inv_ready", "prob_ok", "probT_mm",
                             "probT_sb"))
        map_loaded, out_mm, out_sb, y_mm, res_ok, max_steps, pool_steps, value_hi, front_hi = (
            sem(s) for s in ("map_loaded", "out_mm", "out_sb", "y_mm", "res_ok", "max_steps", "pool_steps",
                             "value_hi", "front_hi"))

        hf, hv = ([ctx.enter_context(nc.sbuf_tensor(f"{name}_{k}{layer}", [P, TOK], F32R)) for k in ("hi", "lo")]
                  for name in ("hf", "hv"))
        v = sb("v", [P, INNER])
        sq = sb("sq", [P, 2 * HEADS, HD])
        ta = sb("ta", [P, 2 * HEADS, HD])
        tb = sb("tb", [P, 2 * HEADS, HD])
        rot = sb("rot", [P, 2 * HEADS, HD])
        ssq = sb("ssq", [P, 2 * HEADS])
        ny = sb("ny", [P, 2 * HEADS])
        nt = sb("nt", [P, 2 * HEADS])
        inv = sb("inv", [P, 2 * HEADS])
        qT = sb("qT", [P, 4, TOK])
        kT = sb("kT", [P, 4, TOK])
        scale = sb("scale", [P, 2, 4])
        mx = sb("mx", [P, 2, 4])
        shift = sb("shift", [P, 2, 4])
        prob = sb("prob", [P, HEADS, TOK])
        total = sb("total", [P, HEADS])
        tinv = sb("tinv", [P, HEADS])
        pT = sb("pT", [P, HEADS, TOK])
        oT = sb("oT", [P, 4, TOK])
        QK, PV, PS, PT, PO = 0, 2, 3, 5, 7
        norm_n = 2 + 3 * NEWTON
        norm_step = [sem(f"norm_step{k}_") for k in range(norm_n)]
        block = ctx.enter_context(nc.Block())

        @block.sync
        def _(sp):
            if layer == 0:
                with sp.Fori(0, SEQS) as s:
                    subject = sp.value_load(m.idx[0:1, 1, bass.ds(s, 1)], min_val=0, max_val=15)
                    sp.dma_start(m.cwc[:, bass.ds(s, 1), :],
                                 a["cwc"][bass.ds(subject, 1), :, :].rearrange("o p n -> p o n"))\
                        .then_inc(map_loaded, 16)
                sp.wait_ge(map_loaded, 16 * SEQS)

        def residual(s):
            return m.res[:, bass.ds(s, 1), 0:TOK].rearrange("p o t -> p (o t)")

        def steps(eng, step):
            for i in range(-2, 2):
                step(i, True, i >= -1, i >= 0, i >= 1)
            with eng.Fori(2, SEQS - 3) as i:
                step(i, True, True, True, True)
            for i in range(SEQS - 3, SEQS + 1):
                step(i, i < SEQS - 2, i < SEQS - 1, i < SEQS, True)

        @block.tensor
        def _(pe):
            def step(i, front, middle, current, back):
                if back:
                    at_least(pe, turned_sb, min(i + 1, SEQS) if isinstance(i, int) else i + 1)
                    for half in range(2):
                        pe.wait_ge(prob_ok, 2 * i - 1 + half)
                        for h in range(4):
                            mm = pe.transpose(m.bank[:, PT + half, h * P:(h + 1) * P], prob[:, 4 * half + h, :],
                                              m.ident[:, :])
                        mm.then_inc(probT_mm, 1)
                if front:
                    pe.wait_ge(front_staged, i + 3)
                    at_least(pe, square_sb, i + 2)
                    for k in range(2):
                        mm = product(pe, m.bank[:, QK + k, :], [h[:, :] for h in hf],
                                     [w[:, layer, k * INNER:(k + 1) * INNER] for w in m.wqkv2])
                    mm.then_inc(qk_mm, 1)
                if back:
                    pe.wait_ge(v_sb, i)
                    pe.wait_ge(probT_sb, 2 * i)
                    at_least(pe, res_ok, i - 1)
                    for c in range(4):
                        for r in range(2):
                            h = 2 * c + r
                            mm = pe.matmul(m.bank[r * HD:(r + 1) * HD, PO, c * P:(c + 1) * P],
                                           v[:, h * HD:(h + 1) * HD], pT[:, 4 * r + c, :], start=True, stop=True)
                    mm.then_inc(out_mm, 1)
                if current:
                    pe.wait_ge(value_staged, i + 1)
                    product(pe, m.bank[:, PV, :], [h[:, :] for h in hv],
                            [w[:, layer, 2 * INNER:] for w in m.wqkv2]).then_inc(v_mm, 1)
                if middle:
                    pe.wait_ge(rotated, i + 2)
                    at_least(pe, probT_sb, 2 * i)
                    for k in range(2):
                        for c in range(4):
                            mm = pe.transpose(m.bank[:, PT + k, c * P:(c + 1) * P],
                                              rot[:, k * HEADS + 2 * c:k * HEADS + 2 * c + 2, :]
                                              .rearrange("p h d -> p (h d)"), m.ident[:, :])
                    mm.then_inc(turn_mm, 1)
                if back:
                    pe.wait_ge(out_sb, i)
                    for c in range(4):
                        mm = pe.matmul(m.bank[:, PO, 0:TOK], m.wo[:, layer, c, :], oT[:, c, :],
                                       start=(c == 0), stop=(c == 3))
                    mm.then_inc(y_mm, 1)
                if middle:
                    at_least(pe, prob_sb, 2 * i + 2)
                    for r in range(2):
                        pe.matmul(m.bank[:, PS + r, :], m.ident16[:, :],
                                  m.mask16[:, :, :].rearrange("p h t -> p (h t)"), start=True, stop=False,
                                  skip_group_check=True)
                    pe.wait_ge(turned_sb, i + 2)
                    for c in range(4):
                        for r in range(2):
                            rows = slice(r * HD, (r + 1) * HD)
                            mm = pe.matmul(m.bank[:, PS + r, c * P:(c + 1) * P], qT[rows, c, :], kT[rows, c, :],
                                           start=False, stop=(c == 3), skip_group_check=True)
                    mm.then_inc(score_mm, 1)
            steps(pe, step)

        @block.scalar
        def _(act):
            def exps(heads):
                for h in heads:
                    last = act.activation(prob[:, h, :], m.bank[:, PS + h // 4, (h % 4) * P:(h % 4 + 1) * P],
                                          ACT.Exp, bias=shift[:, h // 4, h % 4:h % 4 + 1],
                                          scale=scale[:, h // 4, h % 4:h % 4 + 1], accum_out=total[:, h:h + 1])
                return last

            def leading(s, part, last_use, made):
                at_least(act, last_use, s)
                act.copy(part[:, :], residual(s)).then_inc(made, 1)

            leading(0, hf[0], qk_mm, front_hi)

            def step(i, front, middle, current, back):
                if back:
                    at_least(act, out_mm, i - 1)
                    for half in range(2):
                        act.wait_ge(probT_mm, 2 * i - 1 + half)
                        act.copy(pT[:, 4 * half:4 * half + 4, :].rearrange("p h t -> p (h t)"),
                                 m.bank[:, PT + half, :]).then_inc(probT_sb, 1)
                if current:
                    act.wait_ge(shift_ready, i + 1)
                    at_least(act, inv_ready, 2 * i)
                    at_least(act, probT_mm, 2 * i)
                    exps(range(4)).then_inc(prob_sb, 1)
                if back:
                    act.wait_ge(out_mm, i)
                    at_least(act, y_mm, i - 1)
                    act.copy(oT[:, :, :].rearrange("p c t -> p (c t)"), m.bank[:, PO, :]).then_inc(out_sb, 1)
                if current:
                    exps(range(4, HEADS)).then_inc(prob_sb, 1)
                if front:
                    act.wait_ge(rope_k, i + 3)
                    at_least(act, norm_step[0], i + 2)
                    act.activation(sq[:, :, :].rearrange("p h d -> p (h d)"),
                                   m.bank[:, QK:QK + 2, :].rearrange("p k n -> p (k n)"), ACT.Square)\
                        .then_inc(square_sb, 1)
                if current:
                    act.wait_ge(v_mm, i + 1)
                    at_least(act, out_mm, i)
                    act.copy(v[:, :], m.bank[:, PV, :]).then_inc(v_sb, 1)
                if front and not (isinstance(i, int) and i + 3 == SEQS):
                    leading(i + 3, hf[0], qk_mm, front_hi)
                if middle:
                    leading(i + 1, hv[0], v_mm, value_hi)
            steps(act, step)

        @block.gpsimd
        def _(pool):
            def step(i, front, middle, current, back):
                if middle:
                    pool.wait_ge(norm_ready, i + 2)
                    pool.wait_ge(pool_steps, 2 * i + 4)
                    pool.tensor_tensor(rot[:, HEADS:, :], rot[:, HEADS:, :],
                                       inv[:, HEADS:].unsqueeze(2).broadcast_to([P, HEADS, HD]), ALU.mult).then_inc(rotated, 1)
                if current:
                    for half in range(2):
                        pool.wait_ge(inv_ready, 2 * i + 1 + half)
                        heads = slice(4 * half, 4 * half + 4)
                        pool.tensor_tensor(prob[:, heads, :], prob[:, heads, :],
                                           tinv[:, heads].unsqueeze(2).broadcast_to([P, 4, TOK]), ALU.mult)\
                            .then_inc(prob_ok, 1)
                if front:
                    pool.wait_ge(rope_k, i + 3)
                    at_least(pool, turn_mm, i + 2)
                    for k in range(2):
                        pool.tensor_tensor(rot[:, :, k * 32:k * 32 + 32], ta[:, :, k * 32:k * 32 + 32],
                                           tb[:, :, 32 - k * 32:64 - k * 32], ALU.add).then_inc(pool_steps, 1)
            steps(pool, step)

        @block.vector
        def _(dve):
            vec = nc.vector

            def remainder(s, parts, hi_made, made):
                dve.wait_ge(hi_made, s + 1)
                vec.tensor_tensor(parts[1][:, :], residual(s), parts[0][:, :].bitcast(F32), ALU.subtract)\
                    .then_inc(made, 1)

            def rotate(k, n):
                heads = slice(k * HEADS, (k + 1) * HEADS)
                return vec.tensor_tensor((ta, tb)[n][:, heads, :],
                                         m.bank[:, QK + k, :].rearrange("p (h d) -> p h d", d=HD),
                                         m.tab[:, layer, n, k:k + 1, :].broadcast_to([P, HEADS, HD]), ALU.mult)

            def invert(s, half):
                heads = slice(4 * half, 4 * half + 4)
                dve.wait_ge(prob_sb, 2 * s + 1 + half)
                at_least(dve, prob_ok, 2 * s - 1 + half)
                vec.reciprocal(tinv[:, heads], total[:, heads]).then_inc(inv_ready, 1)

            def norm(s, k):
                if k > 0:
                    dve.wait_ge(norm_step[k - 1], s + 1)
                x, y, t = ssq[:, :], ny[:, :], nt[:, :]
                if k == 0:
                    made = vec.tensor_reduce(x, sq[:, :, :], AX.X, ALU.add)
                elif k == 1:
                    made = vec.tensor_scalar(x, x, 1e-24, None, ALU.max)
                elif k == 2:
                    made = vec.tensor_scalar(y.bitcast(I32), x.bitcast(I32), -0.5, RSQRT_MAGIC, ALU.mult, ALU.add)
                elif k % 3 == 0:
                    made = vec.tensor_tensor(t, y, y, ALU.mult)
                elif k % 3 == 1:
                    made = vec.scalar_tensor_tensor(out=t, in0=t, scalar=-0.5, in1=x, op0=ALU.mult, op1=ALU.mult)
                elif k < norm_n:
                    made = vec.scalar_tensor_tensor(out=y, in0=t, scalar=1.5, in1=y, op0=ALU.add, op1=ALU.mult)
                else:
                    at_least(dve, rotated, s)
                    made = vec.scalar_tensor_tensor(out=inv[:, :], in0=t, scalar=1.5, in1=y,
                                                    op0=ALU.add, op1=ALU.mult)
                made.then_inc(norm_ready if k == norm_n else norm_step[k], 1)

            def add_output(s, k):
                dve.wait_ge(y_mm, s + 1)
                rows = slice(k * HALF, (k + 1) * HALF)
                r = m.res[rows, bass.ds(s, 1), k:k + TOK].rearrange("p o t -> p (o t)")
                return vec.tensor_tensor(r, m.bank[rows, PO, 0:TOK], r, ALU.add)

            def step(i, front, middle, current, back):
                before = (not isinstance(i, int)) or i >= 2
                if middle:
                    norm(i + 1, 1)
                if before:
                    add_output(i - 2, 0)
                if middle:
                    norm(i + 1, 2)
                if before:
                    add_output(i - 2, 1).then_inc(res_ok, 1)
                if middle:
                    norm(i + 1, 3)
                if front:
                    remainder(i + 2, hf, front_hi, front_staged)
                if middle:
                    norm(i + 1, 4)
                if current:
                    dve.wait_ge(score_mm, i + 1)
                    at_least(dve, prob_sb, 2 * i)
                    vec.tensor_reduce(mx[:, :, :], m.bank[:, PS:PS + 2, :]
                                      .rearrange("p r (c t) -> p r c t", c=4), AX.X, ALU.max)\
                        .then_inc(max_steps, 1)
                if middle:
                    norm(i + 1, 5)
                if current:
                    vec.tensor_scalar(scale[:, :, :], inv[:, 0:HEADS].rearrange("p (c r) -> p r c", r=2), QK_SCALE, None, ALU.mult)\
                        .then_inc(max_steps, 1)
                if middle:
                    norm(i + 1, 6)
                if current:
                    dve.wait_ge(max_steps, 2 * i + 2)
                    vec.scalar_tensor_tensor(out=shift[:, :, :], in0=mx[:, :, :], scalar=-1.0, in1=scale[:, :, :],
                                             op0=ALU.mult, op1=ALU.mult).then_inc(shift_ready, 1)
                if middle:
                    norm(i + 1, 7)
                if current:
                    remainder(i, hv, value_hi, value_staged)
                if middle:
                    for k in range(8, 12):
                        norm(i + 1, k)
                if front:
                    dve.wait_ge(qk_mm, i + 3)
                    at_least(dve, pool_steps, 2 * i + 4)
                    rotate(0, 0)
                    rotate(0, 1)
                if current:
                    invert(i, 0)
                if front:
                    rotate(1, 0)
                    rotate(1, 1).then_inc(rope_k, 1)
                if middle:
                    dve.wait_ge(turn_mm, i + 2)
                    at_least(dve, score_mm, i + 1)
                    vec.tensor_copy(kT[:, :, :].rearrange("p c t -> p (c t)"), m.bank[:, PT + 1, :])
                    vec.tensor_copy(qT[:, :, :].rearrange("p c t -> p (c t)"), m.bank[:, PT, :]).then_inc(turned_sb, 1)
                if current:
                    invert(i, 1)
                if front:
                    dve.wait_ge(square_sb, i + 3)
                    norm(i + 2, 0)
                if isinstance(i, int) and i == SEQS:
                    add_output(i - 1, 0)
                    add_output(i - 1, 1).then_inc(res_ok, 1)
            steps(dve, step)


def gated_ffn(nc, m, layer):
    with ExitStack() as ctx:
        sem = lambda name: ctx.enter_context(nc.semaphore(f"{name}{layer}"))
        sb = lambda name, shape: ctx.enter_context(nc.sbuf_tensor(f"{name}{layer}", shape, F32))
        staged, rows_mm, rows_sb, turn_mm, turn_sb, turn_lo, up_mm, gelu_sb, gate_sb, down_mm, res_ok, steps_sem = (
            sem(s) for s in ("f_staged", "f_rows_mm", "f_rows_sb", "f_turn_mm", "f_turn_sb", "f_turn_lo", "f_up_mm",
                             "f_gelu_sb", "f_gate_sb", "f_down_mm", "f_res_ok", "f_steps"))
        hs = sb("f_hs", [P, GSEQ, TOK])
        hn = sb("f_hn", [P, GSEQ, DIM])
        hT = [ctx.enter_context(nc.sbuf_tensor(f"f_hT_{k}{layer}", [P, GTOK], F32R)) for k in ("hi", "lo")]
        gelu = sb("f_gelu", [CH, 2, GTOK])
        u = sb("f_u", [CH, NCH, GTOK])
        stats = sb("f_stats", [P, GSEQ, 6])
        mv = sb("f_mv", [P, GSEQ, 2])
        ve = sb("f_ve", [P, GSEQ])
        rstd = sb("f_rstd", [P, GSEQ])
        tmp = sb("f_tmp", [P, GSEQ])
        PR, PT, PU, PD = 0, 1, 2, 6
        block = ctx.enter_context(nc.Block())

        def steps(eng, step):
            step(-1, True, False)
            step(0, True, True)
            with eng.Fori(1, GROUPS - 1) as g:
                step(g, True, True)
            step(GROUPS - 1, False, True)

        @block.tensor
        def _(pe):
            def step(g, norm, products):
                if norm:
                    pe.wait_ge(staged, g + 2)
                    at_least(pe, rows_sb, g + 1)
                    for j in range(GSEQ):
                        mm = pe.transpose(m.bank[:, PR, j * P:(j + 1) * P], hs[:, j, :], m.ident[:, :])
                    mm.then_inc(rows_mm, 1)
                if products:
                    pe.wait_ge(turn_lo, g + 1)
                    for c, (at, n) in enumerate(CHUNKS):
                        at_least(pe, gate_sb, NCH * g + c - 1)
                        for half in range(2):
                            cols = slice(half * HID + at, half * HID + at + n)
                            mm = product(pe, m.bank[0:n, PU + 2 * (c % 2) + half, :],
                                         [w[:, layer, cols] for w in m.w1s], [h[:, :] for h in hT])
                        mm.then_inc(up_mm, 1)
                if norm:
                    pe.wait_ge(rows_sb, g + 2)
                    at_least(pe, turn_lo, g + 1)
                    for j in range(GSEQ):
                        mm = pe.transpose(m.bank[:, PT, j * P:(j + 1) * P], hn[:, j, :], m.ident[:, :])
                    mm.then_inc(turn_mm, 1)
                if products:
                    at_least(pe, res_ok, g)
                    for c, (at, n) in enumerate(CHUNKS):
                        pe.wait_ge(gate_sb, NCH * g + c + 1)
                        mm = pe.matmul(m.bank[:, PD, :], m.w2[0:n, layer, c, :], u[0:n, c, :],
                                       start=(c == 0), stop=(c == NCH - 1))
                    mm.then_inc(down_mm, 1)
            steps(pe, step)

        @block.scalar
        def _(act):
            def step(g, norm, products):
                if products:
                    for c, (_, n) in enumerate(CHUNKS):
                        act.wait_ge(up_mm, NCH * g + c + 1)
                        at_least(act, gate_sb, NCH * g + c - 1)
                        act.activation(gelu[0:n, c % 2, :], m.bank[0:n, PU + 2 * (c % 2) + 1, :], ACT.Gelu,
                                       bias=m.b1eff[0:n, layer, NCH + c:NCH + c + 1]).then_inc(gelu_sb, 1)
                if norm:
                    act.wait_ge(turn_mm, g + 2)
                    at_least(act, up_mm, NCH * (g + 1))
                    act.copy(hT[0][:, :], m.bank[:, PT, :]).then_inc(turn_sb, 1)
            steps(act, step)

        @block.vector
        def _(dve):
            vec = nc.vector

            def step(g, norm, products):
                if norm:
                    at_least(dve, rows_mm, g + 1)
                    vec.tensor_copy(hs[:, :, :], m.res[:, bass.ds((g + 1) * GSEQ, GSEQ), 0:TOK]).then_inc(staged, 1)
                    dve.wait_ge(rows_mm, g + 2)
                    chain = Chain(dve, steps_sem, (g + 1) * LN_STEPS)
                    rows = m.bank[:, PR, :].rearrange("p (s d) -> p s d", s=GSEQ)
                    layernorm_stats(vec, chain, rows, stats, mv, ve, rstd, tmp, DIM)
                    at_least(dve, turn_mm, g + 1)
                    for j in range(GSEQ):
                        last = vec.tensor_scalar(hn[:, j, :], rows[:, j, :], mv[:, j, 0:1], rstd[:, j:j + 1],
                                                 ALU.subtract, ALU.mult)
                    last.then_inc(rows_sb, 1)
                if products:
                    for c, (_, n) in enumerate(CHUNKS):
                        dve.wait_ge(gelu_sb, NCH * g + c + 1)
                        at_least(dve, down_mm, g)
                        vec.scalar_tensor_tensor(out=u[0:n, c, :], in0=m.bank[0:n, PU + 2 * (c % 2), :],
                                                 scalar=m.b1eff[0:n, layer, c:c + 1], in1=gelu[0:n, c % 2, :],
                                                 op0=ALU.add, op1=ALU.mult).then_inc(gate_sb, 1)
                if norm:
                    dve.wait_ge(turn_sb, g + 2)
                    vec.tensor_tensor(hT[1][:, :], m.bank[:, PT, :], hT[0][:, :].bitcast(F32), ALU.subtract)\
                        .then_inc(turn_lo, 1)
                if products:
                    dve.wait_ge(down_mm, g + 1)
                    for k in range(2):
                        rows = slice(k * HALF, (k + 1) * HALF)
                        r = m.res[rows, bass.ds(g * GSEQ, GSEQ), k:k + TOK]
                        last = vec.scalar_tensor_tensor(
                            out=r, in0=m.bank[rows, PD, :].rearrange("p (s t) -> p s t", s=GSEQ),
                            scalar=m.cols[rows, 2, layer:layer + 1], in1=r, op0=ALU.add, op1=ALU.add)
                    last.then_inc(res_ok, 1)
            steps(dve, step)


def ternary_mlp(nc, m, a, out):
    with ExitStack() as ctx:
        sem = lambda name: ctx.enter_context(nc.semaphore(name))
        sb = lambda name, shape: ctx.enter_context(nc.sbuf_tensor(name, shape, F32))
        x1_ok, cond_mm, cond_sb, fc_mm, gelu_sb, norm_ok, turn_mm, turn_sb = (
            sem(s) for s in ("l_x1_ok", "l_cond_mm", "l_cond_sb", "l_fc_mm", "l_gelu_sb",
                             "l_norm_ok", "l_turn_mm", "l_turn_sb"))
        proj_mm, sum_ok, back_mm, back_sb, steps_sem = (
            sem(s) for s in ("l_proj_mm", "l_sum_ok", "l_back_mm", "l_back_sb", "l_steps"))
        stored = [sem(f"l_stored{half}") for half in range(2)]
        cT = sb("l_cT", [P, GSEQ, TOK])
        gl = sb("l_gl", [P, GSEQ, FC])
        gT = sb("l_gT", [P, FC // P, GTOK])
        oT = sb("l_oT", [P, GTOK])
        o = sb("l_o", [P, 2, GTOK])
        stats = sb("l_stats", [P, GSEQ, 6])
        mv = sb("l_mv", [P, GSEQ, 2])
        ve = sb("l_ve", [P, GSEQ])
        rstd = sb("l_rstd", [P, GSEQ])
        tmp = sb("l_tmp", [P, GSEQ])
        PC, PF, PT, PP, PB = 0, 1, 3, 5, 6
        block = ctx.enter_context(nc.Block())

        @block.sync
        def _(sp):
            for g in range(GROUPS):
                sp.wait_ge(back_sb, g + 1)
                sp.dma_start(out[GSEQ * g:GSEQ * (g + 1), :, :].rearrange("s t d -> t s d"),
                             o[:, g % 2, :].rearrange("p (s d) -> p s d", s=GSEQ)).then_inc(stored[g % 2], 16)
            for half in stored:
                sp.wait_ge(half, 16 * GROUPS // 2)

        @block.tensor
        def _(pe):
            def up(g):
                pe.wait_ge(x1_ok, g + 1)
                at_least(pe, cond_sb, g)
                for j in range(GSEQ):
                    mm = pe.matmul(m.bank[:, PC, j * P:(j + 1) * P], m.cwc[:, GSEQ * g + j, 0:DIM], m.x1T[:, GSEQ * g + j, :],
                                   start=True, stop=True)
                mm.then_inc(cond_mm, 1)

            def fc(g):
                pe.wait_ge(cond_sb, g + 1)
                for j in range(GSEQ):
                    at_least(pe, gelu_sb, GSEQ * g + j - 1)
                    pe.matmul(m.bank[:, PF + j % 2, :], cT[:, j, :], m.wfT[:, :], start=True, stop=True)\
                        .then_inc(fc_mm, 1)

            def turn(g):
                pe.wait_ge(norm_ok, g + 1)
                for c in range(FC // P):
                    at_least(pe, turn_sb, 4 * g + c - 1)
                    for j in range(GSEQ):
                        mm = pe.transpose(m.bank[:, PT + c % 2, j * P:(j + 1) * P], gl[:, j, c * P:(c + 1) * P],
                                          m.ident[:, :])
                    mm.then_inc(turn_mm, 1)

            def down(g):
                at_least(pe, sum_ok, g)
                for c in range(FC // P):
                    pe.wait_ge(turn_sb, 4 * g + c + 1)
                    mm = pe.matmul(m.bank[:, PP, :], m.wpT[:, c, :], gT[:, c, :], start=(c == 0), stop=(c == 3))
                mm.then_inc(proj_mm, 1)

            def store(g):
                pe.wait_ge(sum_ok, g + 1)
                at_least(pe, back_sb, g)
                for j in range(GSEQ):
                    mm = pe.transpose(m.bank[:, PB, j * P:(j + 1) * P], oT[:, j * P:(j + 1) * P], m.ident[:, :])
                mm.then_inc(back_mm, 1)

            up(0)
            fc(0)
            for g in range(GROUPS):
                if g + 1 < GROUPS:
                    up(g + 1)
                turn(g)
                down(g)
                if g + 1 < GROUPS:
                    fc(g + 1)
                store(g)

        @block.scalar
        def _(act):
            def gelu(g):
                at_least(act, turn_mm, 4 * g)
                for j in range(GSEQ):
                    act.wait_ge(fc_mm, GSEQ * g + j + 1)
                    act.activation(gl[:, j, :], m.bank[:, PF + j % 2, :], ACT.Gelu).then_inc(gelu_sb, 1)

            def scaled(g):
                for c in range(FC // P):
                    act.wait_ge(turn_mm, 4 * g + c + 1)
                    if c == 0:
                        at_least(act, proj_mm, g)
                    act.activation(gT[:, c, :], m.bank[:, PT + c % 2, :], ACT.Identity,
                                   scale=m.ln1[:, 0, c:c + 1], bias=m.ln1[:, 1, c:c + 1]).then_inc(turn_sb, 1)

            gelu(0)
            for g in range(GROUPS):
                scaled(g)
                if g + 1 < GROUPS:
                    gelu(g + 1)
                act.wait_ge(back_mm, g + 1)
                at_least(act, stored[g % 2], 16 * (g // 2))
                act.copy(o[:, g % 2, :], m.bank[:, PB, :]).then_inc(back_sb, 1)

        @block.vector
        def _(dve):
            vec = nc.vector

            def x1(g):
                for k in range(2):
                    rows = slice(k * HALF, (k + 1) * HALF)
                    s = slice(GSEQ * g, GSEQ * (g + 1))
                    last = vec.tensor_tensor(m.x1T[rows, s, :], m.res[rows, s, k:k + TOK], m.xT[rows, s, :], ALU.add)
                last.then_inc(x1_ok, 1)

            def bias(g):
                dve.wait_ge(cond_mm, g + 1)
                at_least(dve, fc_mm, GSEQ * g)
                vec.tensor_tensor(cT[:, :, :], m.bank[:, PC, :].rearrange("p (s t) -> p s t", s=GSEQ),
                                  m.cwc[:, GSEQ * g:GSEQ * (g + 1), DIM:DIM + 1].broadcast_to([P, GSEQ, TOK]),
                                  ALU.add).then_inc(cond_sb, 1)

            def norm(g):
                dve.wait_ge(gelu_sb, GSEQ * (g + 1))
                chain = Chain(dve, steps_sem, g * LN_STEPS)
                layernorm_stats(vec, chain, gl, stats, mv, ve, rstd, tmp, FC)
                for j in range(GSEQ):
                    last = vec.tensor_scalar(gl[:, j, :], gl[:, j, :], mv[:, j, 0:1], rstd[:, j:j + 1],
                                             ALU.subtract, ALU.mult)
                last.then_inc(norm_ok, 1)

            x1(0)
            bias(0)
            x1(1)
            norm(0)
            for g in range(GROUPS):
                if g + 1 < GROUPS:
                    bias(g + 1)
                if g + 2 < GROUPS:
                    x1(g + 2)
                dve.wait_ge(proj_mm, g + 1)
                at_least(dve, back_mm, g)
                vec.tensor_tensor(oT[:, :], m.bank[:, PP, :],
                                  m.x1T[:, GSEQ * g:GSEQ * (g + 1), :].rearrange("p s t -> p (s t)"), ALU.add)\
                    .then_inc(sum_ok, 1)
                if g + 1 < GROUPS:
                    norm(g + 1)


def program(nc, a, out):
    with ExitStack() as ctx:
        m = Memory(nc, ctx)
        prepare_and_adapt(nc, m, a)
        for layer in range(DEPTH):
            attention(nc, m, a, layer)
            gated_ffn(nc, m, layer)
        ternary_mlp(nc, m, a, out)


def shape_constants():
    i, j = np.arange(TOK)[:, None], np.arange(TOK)[None, :]
    masked = (i < j) | (i > j + WINDOW)
    mask = np.where(masked, -1e30, 0.0).astype(np.float32)
    half = np.arange(0, HD, 2, dtype=np.float32)
    inv_freq = (1.0 / np.float32(10000.0) ** (half / HD)).astype(np.float32)
    t = np.arange(TOK, dtype=np.float32)
    freqs = (t[:, None] * inv_freq[None, :]).astype(np.float32)
    base = ((half + 0.4 * HD) / (1.4 * HD)).astype(np.float32)
    power = ((t - TOK // 2) / float(WINDOW // 2)).astype(np.float32)
    xpos = (base[None, :] ** power[:, None]).astype(np.float32)
    two = lambda z: np.concatenate([z, z], axis=-1)
    cos, sin, xpos = two(np.cos(freqs)), two(np.sin(freqs)), two(xpos)
    sin = sin * np.where(np.arange(HD) < HD // 2, 1.0, -1.0)
    rope = np.stack([np.stack([cos * xpos, cos / xpos], 1), np.stack([sin * xpos, sin / xpos], 1)], 1)
    return {
        "ident": np.eye(P, dtype=np.float32),
        "mask": mask,
        "rope": rope.astype(np.float32),
    }


def kernel(**inputs):
    import concourse.bacc as bacc
    from concourse.bass_utils import run_bass_kernel_spmd

    x = {k: np.asarray(v) for k, v in inputs.items()}
    cond = np.zeros((x["L0_cond_W1"].shape[0], P, COND), np.float32)
    cond[:, :, 0:ADIM] = x["L0_cond_W1"]
    cond[:, 0:ADIM, W2_AT:W2_AT + DIM] = x["L0_cond_W2"]
    cond[:, ADIM, W2_AT:W2_AT + DIM] = x["L0_cond_b2"]
    cond[:, :, GAMMA_AT] = x["L0_cond_gamma"]
    cond[:, :, BETA_AT] = x["L0_cond_beta"]
    cond[:, 0:ADIM, B1_AT] = x["L0_cond_b1"]
    arrays = {
        "x": x["x"], "idx": np.stack([x["itok_B_0_8"], x["itok_B_0_15"]]), "cond": cond,
        "cwc": np.concatenate([x["L1_cond_weights"], x["L1_cond_b"][:, :, None]], axis=2),
        "wqkv": x["L0_ffn_wqkv"], "wo": x["L0_ffn_wo"], "w1": x["L0_ffn_w1"], "w2": x["L0_ffn_w2"],
        "b1": x["L0_ffn_b1"], "b2": x["L0_ffn_b2"], "ln_g0": x["L0_ffn_ln_g"], "ln_b0": x["L0_ffn_ln_b"],
        "qks": np.stack([x["L0_ffn_q_scale"], x["L0_ffn_k_scale"]], axis=1).reshape(-1),
        "W_fc": x["L1_ffn_W_fc"], "W_proj": x["L1_ffn_W_proj"], "ln_w": x["L1_ffn_ln_w"], "ln_b": x["L1_ffn_ln_b"],
    }
    arrays |= shape_constants()
    nc = bacc.Bacc("TRN2", target_bir_lowering=False, num_devices=1)
    feed, aps = {}, {}
    for name, value in arrays.items():
        value = np.ascontiguousarray(value)
        feed[f"in_{name}"] = value
        aps[name] = nc.dram_tensor(f"in_{name}", value.shape, mybir.dt.from_np(value.dtype),
                                   kind="ExternalInput").ap()
    out = nc.dram_tensor("out_0", (SEQS, TOK, DIM), F32, kind="ExternalOutput").ap()
    program(nc, aps, out)
    return run_bass_kernel_spmd(nc, [feed], core_ids=[0]).results[0]["out_0"]
```

```python
import itertools
from contextlib import ExitStack

import numpy as np

import concourse.bass as bass
from concourse import mybir

F32 = mybir.dt.float32
BF16 = mybir.dt.bfloat16
I32 = mybir.dt.int32
F32R = mybir.dt.float32r
ACT = mybir.ActivationFunctionType
ALU = mybir.AluOpType
AX = mybir.AxisListType

P = 128
SEQS, TOK, DIM = 16, 128, 128
HALF = DIM // 2
HEADS, HD = 8, 64
INNER = HEADS * HD
DEPTH = 2
HID = int(DIM * 4 * 2 / 3)
NCH = 3
CH = -(-HID // NCH)
CHUNKS = [(c * CH, min(CH, HID - c * CH)) for c in range(NCH)]
ADIM = 32
FC = 512
W2_AT, GAMMA_AT, BETA_AT, B1_AT, COND = ADIM, ADIM + DIM, ADIM + DIM + 1, ADIM + DIM + 2, ADIM + DIM + 3
GSEQ = 4
GROUPS = SEQS // GSEQ
GTOK = GSEQ * TOK
SKEW = 130
WINDOW = 64
QK_SCALE = 8.0
LN_EPS = 1e-5
RSQRT_MAGIC = float(0x5F3759DF)
NEWTON = 3


class Chain:

    def __init__(self, eng, sem, base):
        self.eng, self.sem, self.base, self.n = eng, sem, base, 0

    def add(self, instruction):
        instruction.then_inc(self.sem, 1)
        self.n += 1

    def wait(self, upto=None):
        self.eng.wait_ge(self.sem, self.base + (self.n if upto is None else upto))


def rsqrt(vec, chain, x, y, t, between=iter(())):
    def wait():
        upto = chain.n
        next(between, None)
        chain.wait(upto)

    chain.add(vec.tensor_scalar(y.bitcast(I32), x.bitcast(I32), -0.5, RSQRT_MAGIC, ALU.mult, ALU.add))
    for _ in range(NEWTON):
        wait()
        chain.add(vec.tensor_tensor(t, y, y, ALU.mult))
        wait()
        chain.add(vec.scalar_tensor_tensor(out=t, in0=t, scalar=-0.5, in1=x, op0=ALU.mult, op1=ALU.mult))
        wait()
        chain.add(vec.scalar_tensor_tensor(out=y, in0=t, scalar=1.5, in1=y, op0=ALU.add, op1=ALU.mult))
    chain.wait()


def product(pe, out, left, right):
    (lh, ll), (rh, rl) = left, right
    pe.matmul(out, lh, rh, start=True, stop=False)
    pe.matmul(out, lh, rl, start=False, stop=False)
    return pe.matmul(out, ll, rh, start=False, stop=True)


def at_least(eng, sem, value):
    if not isinstance(value, int) or value > 0:
        eng.wait_ge(sem, value)


class StageSemaphores:

    def __init__(self, nc, ctx):
        self.nc, self.ctx, self.made = nc, ctx, {}

    def __call__(self, name):
        if name not in self.made:
            self.made[name] = self.ctx.enter_context(self.nc.semaphore(name))
        return self.made[name]

    def clear(self, eng):
        for made in self.made.values():
            eng.sem_clear(made)


class Memory:

    def __init__(self, nc, ctx):
        def sb(name, shape, dt=F32):
            return ctx.enter_context(nc.sbuf_tensor(name, shape, dt))

        self.bank = ctx.enter_context(nc.psum_tensor("bank", [P, 8, 512], F32))
        self.ident = sb("ident", [P, P])
        self.ident16 = sb("ident16", [P, P], BF16)
        self.mask16 = sb("mask16", [P, 4, TOK], BF16)
        self.mask = sb("mask", [P, TOK])
        self.rope = sb("rope", [P, 2, 2, HD])
        self.ones = sb("ones", [P, P])
        self.x_in = sb("x_in", [P, SEQS, DIM])
        self.xT = sb("xT", [P, SEQS, TOK])
        self.res = sb("res", [P, SEQS, SKEW])
        self.x1T = sb("x1T", [P, SEQS, TOK])
        self.hn = sb("hn", [P, SEQS, DIM])
        self.stats = sb("stats", [P, SEQS, 6])
        self.mv = sb("mv", [P, SEQS, 2])
        self.ve = sb("ve", [P, SEQS])
        self.rstd = sb("rstd", [P, SEQS])
        self.tmp = sb("tmp", [P, SEQS])
        self.idx = sb("idx", [1, 2, SEQS], I32)
        self.cond = sb("cond", [P, SEQS, COND])
        self.cwc = sb("cwc", [P, SEQS, DIM + 1])
        self.wqkv = sb("wqkv", [P, DEPTH, 3 * INNER])
        self.wqkv2 = [sb(f"wqkv_{k}", [P, DEPTH, 3 * INNER], F32R) for k in ("hi", "lo")]
        self.wo = sb("wo", [P, DEPTH, INNER // P, DIM])
        self.w1 = sb("w1", [P, DEPTH, 2 * HID])
        self.w1s = [sb(f"w1_{k}", [P, DEPTH, 2 * HID], F32R) for k in ("hi", "lo")]
        self.w2 = sb("w2", [CH, DEPTH, NCH, DIM])
        self.b1 = sb("b1", [CH, DEPTH, 2 * NCH])
        self.b1eff = sb("b1eff", [CH, DEPTH, 2 * NCH])
        self.cols = sb("cols", [P, 3, DEPTH])
        self.qks = sb("qks", [P, DEPTH, 2, HD])
        self.tab = sb("tab", [P, DEPTH, 2, 2, HD])
        self.wf = sb("wf", [P, 2, FC])
        self.wneg = sb("wneg", [P, 2, FC])
        self.wfT = sb("wfT", [P, FC], F32R)
        self.wpT = sb("wpT", [P, FC // P, DIM], F32R)
        self.ln1 = sb("ln1", [P, 2, FC // P])
        self.absum = sb("absum", [P, 2])
        self.thr = sb("thr", [P, 2])


def prepare_and_adapt(nc, m, a, upcoming):
    with ExitStack() as ctx:
        sem = lambda name: ctx.enter_context(nc.semaphore(name))
        sb = lambda name, shape: ctx.enter_context(nc.sbuf_tensor(name, shape, F32))
        idx_loaded, const_loaded, table_loaded, tern_loaded, qkv_loaded, w1_loaded, rest_loaded = (
            sem(s) for s in ("idx_loaded", "const_loaded", "table_loaded", "tern_loaded", "qkv_loaded",
                             "w1_loaded", "rest_loaded"))
        x_loaded = [sem(f"x_loaded{g}") for g in range(GROUPS)]
        cond_loaded = [[sem(f"cond_loaded{g}_{q}") for q in ("sp", "pool")] for g in range(GROUPS)]
        filled, one_row, split_lo, tables, sums, sum_all, ternary, turned, b1_mm, split, scaled, w1_hi, prep_steps = (
            sem(s) for s in ("filled", "one_row", "split_lo", "tables", "sums", "sum_all", "ternary", "turned",
                             "b1_mm", "split", "scaled", "w1_hi", "prep_steps"))
        xt_mm, xt_sb, h1_mm, h1_sb, ad_mm, sum_sb, xn_sb, xn_mm, res_sb, stat_steps = (
            sem(s) for s in ("xt_mm", "xt_sb", "h1_mm", "h1_sb", "ad_mm", "sum_sb", "xn_sb", "xn_mm", "res_sb",
                             "stat_steps"))
        h1 = sb("h1", [ADIM + 1, 2, GSEQ, TOK])
        xr = sb("xr", [P, SEQS, DIM])
        stats = sb("c_stats", [P, SEQS, 6])
        mv = sb("c_mv", [P, SEQS, 2])
        ve = sb("c_ve", [P, SEQS])
        rstd = sb("c_rstd", [P, SEQS])
        tmp = sb("c_tmp", [P, SEQS])
        PX, PH, PA, PN = 0, 2, 4, 6
        block = ctx.enter_context(nc.Block())

        def load_cond(eng, g, j):
            s = GSEQ * g + j
            lang = eng.value_load(m.idx[0:1, 0, s:s + 1], min_val=0, max_val=9)
            eng.dma_start(m.cond[:, s:s + 1, :], a["cond"][bass.ds(lang, 1), :, :].rearrange("o p n -> p o n"))\
                .then_inc(cond_loaded[g][j // 2], 16)

        @block.sync
        def _(sp):
            sp.dma_start(m.idx[:, :, :], a["idx"].rearrange("k (o s) -> o k s", o=1)).then_inc(idx_loaded, 16)
            sp.dma_start(m.ident[:, :], a["ident"]).then_inc(const_loaded, 16)
            sp.wait_ge(idx_loaded, 16)
            for g in range(GROUPS):
                for j in range(2):
                    load_cond(sp, g, j)
            sp.dma_start(m.wqkv[:, :, :], a["wqkv"].rearrange("l p n -> p l n")).then_inc(qkv_loaded, 16)
            for dst, name in ((m.mask[:, :], "mask"), (m.rope[:, :, :, :], "rope")):
                sp.dma_start(dst, a[name]).then_inc(table_loaded, 16)
            sp.dma_start(m.qks[:, :, :, :].rearrange("p l t d -> p (l t d)"),
                         a["qks"].partition_broadcast(P)).then_inc(table_loaded, 16)
            sp.dma_start(m.w1[:, :, :], a["w1"].rearrange("l p n -> p l n")).then_inc(w1_loaded, 16)
            for k, name in enumerate(("ln_g0", "ln_b0", "b2")):
                sp.dma_start(m.cols[:, k, :], a[name].rearrange("l p -> p l"),
                             allow_slow_non_contiguous=True).then_inc(w1_loaded, 16)
            for c, (at, n) in enumerate(CHUNKS):
                for half in range(2):
                    sp.dma_start(m.b1[0:n, :, half * NCH + c],
                                 a["b1"][:, half * HID + at:half * HID + at + n].rearrange("l p -> p l"),
                                 allow_slow_non_contiguous=True).then_inc(w1_loaded, 16)
            sp.dma_start(m.wo[:, :, :, :], a["wo"].rearrange("l (c p) n -> p l c n", p=P)).then_inc(rest_loaded, 16)
            for c, (at, n) in enumerate(CHUNKS):
                sp.dma_start(m.w2[0:n, :, c, :], a["w2"][:, at:at + n, :].rearrange("l p n -> p l n"))\
                    .then_inc(rest_loaded, 16)
            for k, name in enumerate(("ln_w", "ln_b")):
                sp.dma_start(m.ln1[:, k, :], a[name].rearrange("(c p) -> p c", p=P),
                             allow_slow_non_contiguous=True).then_inc(rest_loaded, 16)
            sp.wait_ge(rest_loaded, 16 * (3 + NCH))

        @block.gpsimd
        def _(pool):
            pool.memset(m.ones[:, :], 1.0).then_inc(filled, 1)
            pool.wait_ge(idx_loaded, 16)
            for g in range(GROUPS):
                for j in range(2, GSEQ):
                    load_cond(pool, g, j)
                if g == 0:
                    pool.wait_ge(filled, 1)
                    pool.memset(m.res[:, :, :], 0.0).then_inc(filled, 1)
            for layer in range(DEPTH):
                pool.wait_ge(split, layer + 1)
                at_least(pool, split_lo, layer)
                pool.tensor_tensor(m.wqkv2[1][:, layer, :], m.wqkv[:, layer, :],
                                   m.wqkv2[0][:, layer, :].bitcast(F32), ALU.subtract).then_inc(split_lo, 1)
            for layer in range(DEPTH):
                pool.wait_ge(w1_hi, layer + 1)
                pool.wait_ge(split_lo, DEPTH + layer)
                pool.tensor_tensor(m.w1s[1][:, layer, :], m.w1[:, layer, :], m.w1s[0][:, layer, :].bitcast(F32),
                                   ALU.subtract).then_inc(split_lo, 1)
            pool.wait_ge(split_lo, 2 * DEPTH)
            Attention.first_step(upcoming.gpsimd(pool))

        @block.tensor
        def _(pe):
            def turn_x(g):
                pe.wait_ge(x_loaded[g], 16)
                at_least(pe, xt_sb, g - 1)
                for j in range(GSEQ):
                    mm = pe.transpose(m.bank[:, PX + g % 2, j * P:(j + 1) * P], m.x_in[:, GSEQ * g + j, :],
                                      m.ident[:, :])
                mm.then_inc(xt_mm, 1)

            def down_project(g):
                pe.wait_ge(xt_sb, g + 1)
                for loaded in cond_loaded[g]:
                    pe.wait_ge(loaded, 16 * GSEQ // 2)
                at_least(pe, h1_sb, g - 1)
                for j in range(GSEQ):
                    mm = pe.matmul(m.bank[0:ADIM, PH + g % 2, j * P:(j + 1) * P], m.cond[:, GSEQ * g + j, 0:ADIM],
                                   m.xT[:, GSEQ * g + j, :], start=True, stop=True)
                mm.then_inc(h1_mm, 1)

            def up_project(g):
                pe.wait_ge(h1_sb, g + 1)
                at_least(pe, sum_sb, g - 1)
                for j in range(GSEQ):
                    mm = pe.matmul(m.bank[:, PA + g % 2, j * P:(j + 1) * P], h1[:, g % 2, j, :],
                                   m.cond[0:ADIM + 1, GSEQ * g + j, W2_AT:W2_AT + DIM], start=True, stop=True)
                mm.then_inc(ad_mm, 1)

            def turn_back(g):
                pe.wait_ge(xn_sb, g + 1)
                at_least(pe, res_sb, g - 1)
                for j in range(GSEQ):
                    mm = pe.transpose(m.bank[:, PN + g % 2, j * P:(j + 1) * P], xr[:, GSEQ * g + j, :],
                                      m.ident[:, :])
                mm.then_inc(xn_mm, 1)

            pe.wait_ge(const_loaded, 16)
            turn_x(0)
            turn_x(1)
            pe.wait_ge(filled, 1)
            pe.wait_ge(sums, 2)
            pe.matmul(m.bank[:, PN, 0:2], m.ones[:, :], m.absum[:, :], start=True, stop=True).then_inc(sum_all, 1)
            down_project(0)
            turn_x(2)
            down_project(1)
            pe.wait_ge(one_row, 1)
            up_project(0)
            turn_x(3)
            down_project(2)
            up_project(1)
            down_project(3)
            up_project(2)
            up_project(3)
            pe.wait_ge(ternary, 1)
            for k in range(2):
                for c in range(4):
                    mm = pe.transpose(m.bank[:, PX + k, c * P:(c + 1) * P], m.wf[:, k, c * P:(c + 1) * P],
                                      m.ident[:, :])
            mm.then_inc(turned, 1)
            turn_back(0)
            turn_back(1)
            pe.wait_ge(w1_loaded, 16 * (4 + 2 * NCH))
            for layer in range(DEPTH):
                for k in range(2 * NCH):
                    at, n = CHUNKS[k % NCH]
                    at += (k // NCH) * HID
                    mm = pe.matmul(m.bank[0:n, PH, layer * 2 * NCH + k:layer * 2 * NCH + k + 1],
                                   m.w1[:, layer, at:at + n], m.cols[:, 1, layer:layer + 1],
                                   start=True, stop=True)
            mm.then_inc(b1_mm, 1)
            pe.wait_ge(split_lo, 1)
            Attention.first_step(upcoming.tensor(pe))
            turn_back(2)
            turn_back(3)

        @block.scalar
        def _(act):
            for g in range(GROUPS):
                act.dma_start(m.x_in[:, GSEQ * g:GSEQ * (g + 1), :],
                              a["x"][GSEQ * g:GSEQ * (g + 1), :, :].rearrange("s t d -> t s d"))\
                    .then_inc(x_loaded[g], 16)
            act.dma_start(m.wf[:, 0, :].rearrange("p (c n) -> p c n", c=4),
                          a["W_fc"].rearrange("(c p) n -> p c n", p=P)).then_inc(tern_loaded, 16)
            act.dma_start(m.wf[:, 1, :], a["W_proj"]).then_inc(tern_loaded, 16)

            def copy_x(g):
                act.wait_ge(xt_mm, g + 1)
                act.copy(m.xT[:, GSEQ * g:GSEQ * (g + 1), :].rearrange("p s t -> p (s t)"),
                         m.bank[:, PX + g % 2, :]).then_inc(xt_sb, 1)

            def relu(g):
                act.wait_ge(h1_mm, g + 1)
                at_least(act, ad_mm, g - 1)
                for j in range(GSEQ):
                    last = act.activation(h1[0:ADIM, g % 2, j, :], m.bank[0:ADIM, PH + g % 2, j * P:(j + 1) * P],
                                          ACT.Relu, bias=m.cond[0:ADIM, GSEQ * g + j, B1_AT:B1_AT + 1])
                last.then_inc(h1_sb, 1)

            def residual_of(g):
                act.wait_ge(xn_mm, g + 1)
                for j in range(GSEQ):
                    s = GSEQ * g + j
                    for k in range(2):
                        rows = slice(k * HALF, (k + 1) * HALF)
                        last = act.activation(m.res[rows, s, k:k + TOK],
                                              m.bank[rows, PN + g % 2, j * P:(j + 1) * P], ACT.Identity,
                                              scale=m.cond[rows, s, GAMMA_AT:GAMMA_AT + 1],
                                              bias=m.cond[rows, s, BETA_AT:BETA_AT + 1])
                last.then_inc(res_sb, 1)

            copy_x(0)
            copy_x(1)
            relu(0)
            copy_x(2)
            relu(1)
            copy_x(3)
            relu(2)
            relu(3)
            act.wait_ge(qkv_loaded, 16)
            for layer in range(DEPTH):
                act.copy(m.wqkv2[0][:, layer, :], m.wqkv[:, layer, :]).then_inc(split, 1)
            act.wait_ge(turned, 1)
            act.copy(m.wfT[:, :], m.bank[:, PX, :])
            act.copy(m.wpT[:, :, :].rearrange("p c n -> p (c n)"), m.bank[:, PX + 1, :])
            act.wait_ge(filled, 2)
            residual_of(0)
            act.wait_ge(res_sb, 1)
            upcoming.split_hi(act)
            residual_of(1)
            for layer in range(DEPTH):
                act.wait_ge(scaled, layer + 1)
                act.copy(m.w1s[0][:, layer, :], m.w1[:, layer, :]).then_inc(w1_hi, 1)
            residual_of(2)
            Attention.first_step(upcoming.scalar(act))
            residual_of(3)

        @block.vector
        def _(dve):
            vec = nc.vector
            chain = Chain(dve, prep_steps, 0)
            vec.memset(h1[ADIM:ADIM + 1, :, :, :], 1.0).then_inc(one_row, 1)
            dve.wait_ge(tern_loaded, 16 * 2)
            for k in range(2):
                vec.tensor_reduce(m.absum[:, k:k + 1], m.wf[:, k, :], AX.X, ALU.add, apply_absolute_value=True)\
                    .then_inc(sums, 1)
            dve.wait_ge(sum_all, 1)
            chain.add(vec.tensor_scalar(m.thr[:, :], m.bank[:, PN, 0:2], 1.0 / (FC * DIM), 1e-6,
                                        ALU.mult, ALU.add))
            chain.wait()
            chain.add(vec.tensor_scalar(m.thr[:, :], m.thr[:, :], 0.5, None, ALU.mult))
            chain.wait()
            for k in range(2):
                chain.add(vec.tensor_scalar(m.wneg[:, k, :], m.wf[:, k, :], -1.0, m.thr[:, k:k + 1],
                                            ALU.mult, ALU.is_gt))
            chain.wait()
            for k in range(2):
                last = vec.scalar_tensor_tensor(out=m.wf[:, k, :], in0=m.wf[:, k, :], scalar=m.thr[:, k:k + 1],
                                                in1=m.wneg[:, k, :], op0=ALU.is_gt, op1=ALU.subtract)
            last.then_inc(ternary, 1)

            norm_chain = Chain(dve, stat_steps, 0)

            def add_adapter(g):
                dve.wait_ge(ad_mm, g + 1)
                s = slice(GSEQ * g, GSEQ * (g + 1))
                vec.tensor_tensor(xr[:, s, :].rearrange("p s t -> p (s t)"), m.bank[:, PA + g % 2, :],
                                  m.x_in[:, s, :].rearrange("p s t -> p (s t)"), ALU.add).then_inc(sum_sb, 1)
                dve.wait_ge(sum_sb, g + 1)
                row_stats(vec, norm_chain, xr[:, s, :], stats[:, s, :])

            def normalise(g, between):
                s = slice(GSEQ * g, GSEQ * (g + 2))
                inverse_deviation(vec, norm_chain, stats[:, s, :], mv[:, s, :], ve[:, s], rstd[:, s], tmp[:, s],
                                  DIM, between)
                for h in (g, g + 1):
                    for t in range(GSEQ * h, GSEQ * (h + 1)):
                        last = vec.tensor_scalar(xr[:, t, :], xr[:, t, :], mv[:, t, 0:1], rstd[:, t:t + 1],
                                                 ALU.subtract, ALU.mult)
                    last.then_inc(xn_sb, 1)

            def copy_constants():
                dve.wait_ge(const_loaded, 16)
                dve.wait_ge(table_loaded, 16 * 3)
                yield vec.tensor_copy(m.ident16[:, :], m.ident[:, :])
                yield vec.tensor_copy(m.mask16[:, :, :], m.mask[:, :].unsqueeze(1).broadcast_to([P, 4, TOK]))

            def prepare_tables(layer):
                for k in range(2):
                    yield vec.tensor_tensor(m.tab[:, layer, k, :, :], m.rope[:, k, :, :],
                                            m.qks[:, layer, :, :], ALU.mult).then_inc(tables, 1)

            def prepare_w1():
                dve.wait_ge(b1_mm, 1)
                for layer in range(DEPTH):
                    yield vec.tensor_scalar(m.w1[:, layer, :], m.w1[:, layer, :], m.cols[:, 0, layer:layer + 1],
                                            None, ALU.mult).then_inc(scaled, 1)
                for layer in range(DEPTH):
                    for k in range(2 * NCH):
                        n = CHUNKS[k % NCH][1]
                        yield vec.tensor_tensor(m.b1eff[0:n, layer, k:k + 1],
                                                m.bank[0:n, PH, layer * 2 * NCH + k:layer * 2 * NCH + k + 1],
                                                m.b1[0:n, layer, k:k + 1], ALU.add)

            def split_first():
                yield upcoming.split_lo(dve)

            add_adapter(0)
            add_adapter(1)
            normalise(0, copy_constants())
            add_adapter(2)
            add_adapter(3)
            rest = itertools.chain(*(prepare_tables(layer) for layer in range(DEPTH)), split_first(), prepare_w1())
            normalise(2, rest)
            complete(rest)
            dve.wait_ge(tables, 2 * DEPTH)
            Attention.first_step(upcoming.vector(dve))


def row_stats(vec, chain, rows, stats):
    for j in range(rows.shape[1]):
        chain.add(vec.bn_stats(stats[:, j, :], rows[:, j, :]))


def inverse_deviation(vec, chain, stats, mv, ve, rstd, tmp, width, between=iter(())):
    chain.wait()
    (me, qe), (mo, qo) = ((stats[:, :, 3 * k + 1], stats[:, :, 3 * k + 2]) for k in range(2))
    mean = mv[:, :, 0]
    chain.add(vec.tensor_tensor(mean, me, mo, ALU.add))
    chain.add(vec.tensor_tensor(tmp, me, mo, ALU.subtract))
    chain.add(vec.tensor_tensor(ve, qe, qo, ALU.add))
    upto = chain.n
    next(between, None)
    chain.wait(upto)
    chain.add(vec.tensor_scalar(mean, mean, 0.5, None, ALU.mult))
    chain.add(vec.scalar_tensor_tensor(out=tmp, in0=tmp, scalar=0.25, in1=tmp, op0=ALU.mult, op1=ALU.mult))
    chain.add(vec.tensor_scalar(ve, ve, 1.0 / width, LN_EPS, ALU.mult, ALU.add))
    upto = chain.n
    next(between, None)
    chain.wait(upto)
    chain.add(vec.tensor_tensor(ve, ve, tmp, ALU.add))
    upto = chain.n
    next(between, None)
    chain.wait(upto)
    rsqrt(vec, chain, ve, rstd, tmp, between)


def complete(pieces):
    for _ in pieces:
        pass


def group_rows(m, bank):
    return m.bank[:, bank, :].rearrange("p (s d) -> p s d", s=GSEQ)


def turn_rows(pe, m, g, bank):
    for j in range(GSEQ):
        mm = pe.transpose(m.bank[:, bank, j * P:(j + 1) * P], m.res[:, GSEQ * g + j, 0:TOK], m.ident[:, :])
    return mm


def pair_deviation(vec, chain, m, g, between=iter(())):
    s = slice(GSEQ * g, GSEQ * (g + 2))
    inverse_deviation(vec, chain, m.stats[:, s, :], m.mv[:, s, :], m.ve[:, s], m.rstd[:, s], m.tmp[:, s], DIM,
                      between)


def normalise_rows(vec, m, g, bank):
    for j in range(GSEQ):
        s = GSEQ * g + j
        last = vec.tensor_scalar(m.hn[:, s, :], group_rows(m, bank)[:, j, :], m.mv[:, s, 0:1], m.rstd[:, s:s + 1],
                                 ALU.subtract, ALU.mult)
    return last


class AttentionBuffers:

    def __init__(self, nc, ctx):
        def sb(name, shape, dt=F32):
            return ctx.enter_context(nc.sbuf_tensor(name, shape, dt))

        self.hf, self.hv = ([sb(f"{name}_{k}", [P, TOK], F32R) for k in ("hi", "lo")] for name in ("hf", "hv"))
        self.v = sb("v", [P, INNER])
        self.sq, self.ta, self.tb, self.rot = (sb(name, [P, 2 * HEADS, HD]) for name in ("sq", "ta", "tb", "rot"))
        self.ssq, self.ny, self.nt, self.inv = (sb(name, [P, 2 * HEADS]) for name in ("ssq", "ny", "nt", "inv"))
        self.qkT = sb("qkT", [P, 2, 4, TOK])
        self.oT = sb("oT", [P, 4, TOK])
        self.scale, self.mx, self.shift = (sb(name, [P, 2, 4]) for name in ("scale", "mx", "shift"))
        self.prob, self.pT = (sb(name, [P, HEADS, TOK]) for name in ("prob", "pT"))
        self.total, self.tinv = (sb(name, [P, HEADS]) for name in ("total", "tinv"))


class Attention:

    def __init__(self, nc, ctx, m, buf, layer):
        sem = lambda name: ctx.enter_context(nc.semaphore(f"{name}{layer}"))
        front_staged, value_staged, qk_mm, v_mm, v_sb = (
            sem(s) for s in ("front_staged", "value_staged", "qk_mm", "v_mm", "v_sb"))
        square_sb, rope_k, norm_ready, rotated, turn_mm, turned_sb = (
            sem(s) for s in ("square_sb", "rope_k", "norm_ready", "rotated", "turn_mm", "turned_sb"))
        score_mm, shift_ready, prob_sb, inv_ready, prob_ok, probT_mm, probT_sb = (
            sem(s) for s in ("score_mm", "shift_ready", "prob_sb", "inv_ready", "prob_ok", "probT_mm",
                             "probT_sb"))
        out_mm, out_sb, y_mm, res_ok, max_steps, pool_steps, value_hi, front_hi, tail_mm, tail_steps = (
            sem(s) for s in ("out_mm", "out_sb", "y_mm", "res_ok", "max_steps", "pool_steps", "value_hi",
                             "front_hi", "tail_mm", "tail_steps"))

        hf, hv, v, sq, ta, tb, rot = buf.hf, buf.hv, buf.v, buf.sq, buf.ta, buf.tb, buf.rot
        ssq, ny, nt, inv, qkT, oT = buf.ssq, buf.ny, buf.nt, buf.inv, buf.qkT, buf.oT
        scale, mx, shift, prob, pT, total, tinv = (buf.scale, buf.mx, buf.shift, buf.prob, buf.pT, buf.total,
                                                   buf.tinv)
        QK, PV, PS, PT, PO = 0, 2, 3, 5, 7
        norm_n = 2 + 3 * NEWTON
        norm_step = [sem(f"norm_step{k}_") for k in range(norm_n)]
        def residual(s):
            return m.res[:, bass.ds(s, 1), 0:TOK].rearrange("p o t -> p (o t)")

        def split_hi(act):
            act.copy(hf[0][:, :], m.res[:, 0, 0:TOK]).then_inc(front_hi, 1)

        def split_lo(dve):
            dve.wait_ge(front_hi, 1)
            nc.vector.tensor_tensor(hf[1][:, :], m.res[:, 0, 0:TOK], hf[0][:, :].bitcast(F32), ALU.subtract)\
                .then_inc(front_staged, 1)

        self.split_hi, self.split_lo = split_hi, split_lo

        def tensor(pe):
            def step(i, front, middle, current, back):
                if back:
                    at_least(pe, turned_sb, min(i + 1, SEQS) if isinstance(i, int) else i + 1)
                    for half in range(2):
                        pe.wait_ge(prob_ok, 2 * i - 1 + half)
                        for h in range(4):
                            mm = pe.transpose(m.bank[:, PT + half, h * P:(h + 1) * P], prob[:, 4 * half + h, :],
                                              m.ident[:, :])
                        mm.then_inc(probT_mm, 1)
                if front:
                    pe.wait_ge(front_staged, i + 3)
                    at_least(pe, square_sb, i + 2)
                    for k in range(2):
                        mm = product(pe, m.bank[:, QK + k, :], [h[:, :] for h in hf],
                                     [w[:, layer, k * INNER:(k + 1) * INNER] for w in m.wqkv2])
                    mm.then_inc(qk_mm, 1)
                if back:
                    pe.wait_ge(v_sb, i)
                    pe.wait_ge(probT_sb, 2 * i)
                    at_least(pe, res_ok, i - 1)
                    for c in range(4):
                        for r in range(2):
                            h = 2 * c + r
                            mm = pe.matmul(m.bank[r * HD:(r + 1) * HD, PO, c * P:(c + 1) * P],
                                           v[:, h * HD:(h + 1) * HD], pT[:, 4 * r + c, :], start=True, stop=True)
                    mm.then_inc(out_mm, 1)
                if current:
                    pe.wait_ge(value_staged, i + 1)
                    product(pe, m.bank[:, PV, :], [h[:, :] for h in hv],
                            [w[:, layer, 2 * INNER:] for w in m.wqkv2]).then_inc(v_mm, 1)
                if isinstance(i, int) and i == SEQS - 2:
                    pe.wait_ge(square_sb, SEQS)
                    for g in range(2):
                        turn_rows(pe, m, g, QK + g).then_inc(tail_mm, 1)
                if middle:
                    pe.wait_ge(rotated, i + 2)
                    at_least(pe, probT_sb, 2 * i)
                    for k in range(2):
                        for c in range(4):
                            mm = pe.transpose(m.bank[:, PT + k, c * P:(c + 1) * P],
                                              rot[:, k * HEADS + 2 * c:k * HEADS + 2 * c + 2, :]
                                              .rearrange("p h d -> p (h d)"), m.ident[:, :])
                    mm.then_inc(turn_mm, 1)
                if back:
                    pe.wait_ge(out_sb, i)
                    for c in range(4):
                        mm = pe.matmul(m.bank[:, PO, 0:TOK], m.wo[:, layer, c, :], oT[:, c, :],
                                       start=(c == 0), stop=(c == 3))
                    mm.then_inc(y_mm, 1)
                if middle:
                    at_least(pe, prob_sb, 2 * i + 2)
                    for r in range(2):
                        pe.matmul(m.bank[:, PS + r, :], m.ident16[:, :],
                                  m.mask16[:, :, :].rearrange("p h t -> p (h t)"), start=True, stop=False,
                                  skip_group_check=True)
                    pe.wait_ge(turned_sb, i + 2)
                    for c in range(4):
                        for r in range(2):
                            rows = slice(r * HD, (r + 1) * HD)
                            mm = pe.matmul(m.bank[:, PS + r, c * P:(c + 1) * P], qkT[rows, 0, c, :], qkT[rows, 1, c, :],
                                           start=False, stop=(c == 3), skip_group_check=True)
                    mm.then_inc(score_mm, 1)
            return step

        def scalar(act):
            def exps(heads):
                for h in heads:
                    last = act.activation(prob[:, h, :], m.bank[:, PS + h // 4, (h % 4) * P:(h % 4 + 1) * P],
                                          ACT.Exp, bias=shift[:, h // 4, h % 4:h % 4 + 1],
                                          scale=scale[:, h // 4, h % 4:h % 4 + 1], accum_out=total[:, h:h + 1])
                return last

            def leading(s, part, last_use, made):
                at_least(act, last_use, s)
                act.copy(part[:, :], residual(s)).then_inc(made, 1)

            def step(i, front, middle, current, back):
                if back:
                    at_least(act, out_mm, i - 1)
                    for half in range(2):
                        act.wait_ge(probT_mm, 2 * i - 1 + half)
                        act.copy(pT[:, 4 * half:4 * half + 4, :].rearrange("p h t -> p (h t)"),
                                 m.bank[:, PT + half, :]).then_inc(probT_sb, 1)
                if current:
                    act.wait_ge(shift_ready, i + 1)
                    at_least(act, inv_ready, 2 * i)
                    at_least(act, probT_mm, 2 * i)
                    exps(range(4)).then_inc(prob_sb, 1)
                if back:
                    act.wait_ge(out_mm, i)
                    at_least(act, y_mm, i - 1)
                    act.copy(oT[:, :, :].rearrange("p c t -> p (c t)"), m.bank[:, PO, :]).then_inc(out_sb, 1)
                if current:
                    exps(range(4, HEADS)).then_inc(prob_sb, 1)
                if front:
                    act.wait_ge(rope_k, i + 3)
                    at_least(act, norm_step[0], i + 2)
                    act.activation(sq[:, :, :].rearrange("p h d -> p (h d)"),
                                   m.bank[:, QK:QK + 2, :].rearrange("p k n -> p (k n)"), ACT.Square)\
                        .then_inc(square_sb, 1)
                if current:
                    act.wait_ge(v_mm, i + 1)
                    at_least(act, out_mm, i)
                    act.copy(v[:, :], m.bank[:, PV, :]).then_inc(v_sb, 1)
                if front and not (isinstance(i, int) and i + 3 == SEQS):
                    leading(i + 3, hf[0], qk_mm, front_hi)
                if middle:
                    leading(i + 1, hv[0], v_mm, value_hi)
            return step

        def gpsimd(pool):
            def step(i, front, middle, current, back):
                if middle:
                    pool.wait_ge(norm_ready, i + 2)
                    pool.wait_ge(pool_steps, 2 * i + 4)
                    pool.tensor_tensor(rot[:, HEADS:, :], rot[:, HEADS:, :],
                                       inv[:, HEADS:].unsqueeze(2).broadcast_to([P, HEADS, HD]), ALU.mult)\
                        .then_inc(rotated, 1)
                if current:
                    for half in range(2):
                        pool.wait_ge(inv_ready, 2 * i + 1 + half)
                        heads = slice(4 * half, 4 * half + 4)
                        pool.tensor_tensor(prob[:, heads, :], prob[:, heads, :],
                                           tinv[:, heads].unsqueeze(2).broadcast_to([P, 4, TOK]), ALU.mult)\
                            .then_inc(prob_ok, 1)
                if front:
                    pool.wait_ge(rope_k, i + 3)
                    at_least(pool, turn_mm, i + 2)
                    for k in range(2):
                        pool.tensor_tensor(rot[:, :, k * 32:k * 32 + 32], ta[:, :, k * 32:k * 32 + 32],
                                           tb[:, :, 32 - k * 32:64 - k * 32], ALU.add).then_inc(pool_steps, 1)
            return step

        def vector(dve):
            vec = nc.vector

            def remainder(s, parts, hi_made, made):
                dve.wait_ge(hi_made, s + 1)
                vec.tensor_tensor(parts[1][:, :], residual(s), parts[0][:, :].bitcast(F32), ALU.subtract)\
                    .then_inc(made, 1)

            def rotate(n):
                return vec.tensor_tensor(
                    (ta, tb)[n][:, :, :].rearrange("p (k h) d -> p k h d", k=2),
                    m.bank[:, QK:QK + 2, :].rearrange("p k (h d) -> p k h d", d=HD),
                    m.tab[:, layer, n, :, :].unsqueeze(2).broadcast_to([P, 2, HEADS, HD]), ALU.mult)

            def invert(s, half):
                heads = slice(4 * half, 4 * half + 4)
                dve.wait_ge(prob_sb, 2 * s + 1 + half)
                at_least(dve, prob_ok, 2 * s - 1 + half)
                vec.reciprocal(tinv[:, heads], total[:, heads]).then_inc(inv_ready, 1)

            def norm(s, k):
                if k > 0:
                    dve.wait_ge(norm_step[k - 1], s + 1)
                x, y, t = ssq[:, :], ny[:, :], nt[:, :]
                if k == 0:
                    made = vec.tensor_reduce(x, sq[:, :, :], AX.X, ALU.add)
                elif k == 1:
                    made = vec.tensor_scalar(x, x, 1e-24, None, ALU.max)
                elif k == 2:
                    made = vec.tensor_scalar(y.bitcast(I32), x.bitcast(I32), -0.5, RSQRT_MAGIC, ALU.mult, ALU.add)
                elif k % 3 == 0:
                    made = vec.tensor_tensor(t, y, y, ALU.mult)
                elif k % 3 == 1:
                    made = vec.scalar_tensor_tensor(out=t, in0=t, scalar=-0.5, in1=x, op0=ALU.mult, op1=ALU.mult)
                elif k < norm_n:
                    made = vec.scalar_tensor_tensor(out=y, in0=t, scalar=1.5, in1=y, op0=ALU.add, op1=ALU.mult)
                else:
                    at_least(dve, rotated, s)
                    made = vec.scalar_tensor_tensor(out=inv[:, :], in0=t, scalar=1.5, in1=y,
                                                    op0=ALU.add, op1=ALU.mult)
                made.then_inc(norm_ready if k == norm_n else norm_step[k], 1)

            tail_chain = Chain(dve, tail_steps, 0)

            def add_output(s, k):
                dve.wait_ge(y_mm, s + 1)
                rows = slice(k * HALF, (k + 1) * HALF)
                r = m.res[rows, bass.ds(s, 1), k:k + TOK].rearrange("p o t -> p (o t)")
                return vec.tensor_tensor(r, m.bank[rows, PO, 0:TOK], r, ALU.add)

            def step(i, front, middle, current, back):
                before = (not isinstance(i, int)) or i >= 2
                if middle:
                    norm(i + 1, 1)
                if before:
                    add_output(i - 2, 0)
                if middle:
                    norm(i + 1, 2)
                if front and not (isinstance(i, int) and i == -2):
                    remainder(i + 2, hf, front_hi, front_staged)
                if current:
                    dve.wait_ge(score_mm, i + 1)
                    at_least(dve, prob_sb, 2 * i)
                    vec.tensor_reduce(mx[:, :, :], m.bank[:, PS:PS + 2, :]
                                      .rearrange("p r (c t) -> p r c t", c=4), AX.X, ALU.max)\
                        .then_inc(max_steps, 1)
                if middle:
                    norm(i + 1, 3)
                if current:
                    vec.tensor_scalar(scale[:, :, :], inv[:, 0:HEADS].rearrange("p (c r) -> p r c", r=2),
                                      QK_SCALE, None, ALU.mult).then_inc(max_steps, 1)
                if middle:
                    norm(i + 1, 4)
                if current:
                    dve.wait_ge(max_steps, 2 * i + 2)
                    vec.scalar_tensor_tensor(out=shift[:, :, :], in0=mx[:, :, :], scalar=-1.0, in1=scale[:, :, :],
                                             op0=ALU.mult, op1=ALU.mult).then_inc(shift_ready, 1)
                if middle:
                    norm(i + 1, 5)
                if before:
                    add_output(i - 2, 1).then_inc(res_ok, 1)
                if middle:
                    norm(i + 1, 6)
                if current:
                    remainder(i, hv, value_hi, value_staged)
                if middle:
                    for k in range(7, 12):
                        norm(i + 1, k)
                if front:
                    dve.wait_ge(qk_mm, i + 3)
                    at_least(dve, pool_steps, 2 * i + 4)
                    rotate(0)
                if isinstance(i, int) and i == SEQS - 2:
                    for g in range(2):
                        dve.wait_ge(tail_mm, g + 1)
                        row_stats(vec, tail_chain, group_rows(m, QK + g), m.stats[:, GSEQ * g:GSEQ * (g + 1), :])
                if isinstance(i, int) and i == SEQS - 1:
                    pair_deviation(vec, tail_chain, m, 0)
                if current:
                    invert(i, 0)
                if isinstance(i, int) and i >= SEQS - 1:
                    normalise_rows(vec, m, i - SEQS + 1, QK + i - SEQS + 1)
                if front:
                    rotate(1).then_inc(rope_k, 1)
                if middle:
                    dve.wait_ge(turn_mm, i + 2)
                    at_least(dve, score_mm, i + 1)
                    vec.tensor_copy(qkT[:, :, :, :].rearrange("p k c t -> p k (c t)"), m.bank[:, PT:PT + 2, :])\
                        .then_inc(turned_sb, 1)
                if current:
                    invert(i, 1)
                if front:
                    dve.wait_ge(square_sb, i + 3)
                    norm(i + 2, 0)
                if isinstance(i, int) and i == SEQS:
                    add_output(i - 1, 0)
                    add_output(i - 1, 1).then_inc(res_ok, 1)
            return step

        self.layer = layer
        self.map_loaded = sem("map_loaded")
        self.tensor, self.scalar, self.gpsimd, self.vector = tensor, scalar, gpsimd, vector

    @staticmethod
    def first_step(step):
        step(-2, True, False, False, False)

    @staticmethod
    def later_steps(eng, step):
        for i in range(-1, 2):
            step(i, True, i >= -1, i >= 0, i >= 1)
        with eng.Fori(2, SEQS - 3) as i:
            step(i, True, True, True, True)
        for i in range(SEQS - 3, SEQS + 1):
            step(i, i < SEQS - 2, i < SEQS - 1, i < SEQS, True)

    def run(self, nc, m, a, idle_sems):
        with nc.Block() as block:
            @block.sync
            def _(sp):
                if self.layer > 0:
                    idle_sems.clear(sp)
                else:
                    with sp.Fori(0, SEQS) as s:
                        subject = sp.value_load(m.idx[0:1, 1, bass.ds(s, 1)], min_val=0, max_val=15)
                        sp.dma_start(m.cwc[:, bass.ds(s, 1), :],
                                     a["cwc"][bass.ds(subject, 1), :, :].rearrange("o p n -> p o n"))\
                            .then_inc(self.map_loaded, 16)
                    sp.wait_ge(self.map_loaded, 16 * SEQS)

            @block.tensor
            def _(pe):
                self.later_steps(pe, self.tensor(pe))

            @block.scalar
            def _(act):
                self.later_steps(act, self.scalar(act))

            @block.gpsimd
            def _(pool):
                self.later_steps(pool, self.gpsimd(pool))

            @block.vector
            def _(dve):
                self.later_steps(dve, self.vector(dve))


def add_x(eng, m, g):
    seqs = slice(GSEQ * g, GSEQ * (g + 1))
    for k in range(2):
        rows = slice(k * HALF, (k + 1) * HALF)
        last = eng.tensor_tensor(m.x1T[rows, seqs, :], m.res[rows, seqs, k:k + TOK], m.xT[rows, seqs, :], ALU.add)
    return last


def gated_ffn(nc, m, layer, sem, upcoming):
    with ExitStack() as ctx:
        sb = lambda name, shape, dt=F32: ctx.enter_context(nc.sbuf_tensor(f"{name}{layer}", shape, dt))
        rows_mm, norm_ok, turn_mm, turn_hi, turn_lo, up_mm, gelu_sb, gate_sb = (
            sem(s) for s in ("f_rows_mm", "f_norm_ok", "f_turn_mm", "f_turn_hi", "f_turn_lo",
                             "f_up_mm", "f_gelu_sb", "f_gate_sb"))
        down_mm, res_ok, x1_ok, steps_sem = (sem(s) for s in ("f_down_mm", "f_res_ok", "f_x1_ok", "f_steps"))
        hT = [sb(f"f_hT_{k}", [P, 2, GTOK], F32R) for k in ("hi", "lo")]
        gelu = sb("f_gelu", [CH, 2, GTOK])
        u = sb("f_u", [CH, 2, NCH, GTOK])
        PR, PT, PU, PD = {2: 0, 3: 7}, 1, (2, 4), (6, 7)
        block = ctx.enter_context(nc.Block())

        @block.gpsimd
        def _(pool):
            if upcoming:
                Attention.first_step(upcoming.gpsimd(pool))
            if layer + 1 == DEPTH:
                for g in range(GROUPS - 1):
                    pool.wait_ge(res_ok, g + 1)
                    at_least(pool, x1_ok, g)
                    add_x(pool, m, g).then_inc(x1_ok, 1)

        @block.tensor
        def _(pe):
            def turn(g):
                at_least(pe, norm_ok, g - 1)
                at_least(pe, turn_lo, g)
                for j in range(GSEQ):
                    mm = pe.transpose(m.bank[:, PT, j * P:(j + 1) * P], m.hn[:, GSEQ * g + j, :], m.ident[:, :])
                mm.then_inc(turn_mm, 1)

            def up(g, c):
                n_chunk = NCH * g + c
                pe.wait_ge(turn_lo, g + 1)
                at_least(pe, gate_sb, n_chunk - 1)
                at, n = CHUNKS[c]
                for half in range(2):
                    cols = slice(half * HID + at, half * HID + at + n)
                    mm = product(pe, m.bank[0:n, PU[n_chunk % 2] + half, :],
                                 [w[:, layer, cols] for w in m.w1s], [h[:, g % 2, :] for h in hT])
                mm.then_inc(up_mm, 1)

            def down(g):
                if g == 1:
                    pe.wait_ge(norm_ok, 2)
                at_least(pe, res_ok, g - 1)
                for c, (at, n) in enumerate(CHUNKS):
                    pe.wait_ge(gate_sb, NCH * g + c + 1)
                    mm = pe.matmul(m.bank[:, PD[g % 2], :], m.w2[0:n, layer, c, :], u[0:n, g % 2, c, :],
                                   start=(c == 0), stop=(c == NCH - 1))
                mm.then_inc(down_mm, 1)

            turn(0)
            for g in PR:
                turn_rows(pe, m, g, PR[g]).then_inc(rows_mm, 1)
            for g in range(GROUPS):
                up(g, 0)
                if g > 0:
                    down(g - 1)
                if g + 1 < GROUPS:
                    turn(g + 1)
                elif upcoming:
                    Attention.first_step(upcoming.tensor(pe))
                for c in range(1, NCH):
                    up(g, c)
            down(GROUPS - 1)

        @block.scalar
        def _(act):
            def leading(g):
                act.wait_ge(turn_mm, g + 1)
                at_least(act, up_mm, NCH * (g - 1))
                act.copy(hT[0][:, g % 2, :], m.bank[:, PT, :]).then_inc(turn_hi, 1)

            leading(0)
            for g in range(GROUPS):
                for c, (_, n) in enumerate(CHUNKS):
                    if upcoming and g == GROUPS - 1 and c == 0:
                        act.wait_ge(res_ok, 1)
                        upcoming.split_hi(act)
                    n_chunk = NCH * g + c
                    act.wait_ge(up_mm, n_chunk + 1)
                    at_least(act, gate_sb, n_chunk - 1)
                    act.activation(gelu[0:n, n_chunk % 2, :], m.bank[0:n, PU[n_chunk % 2] + 1, :], ACT.Gelu,
                                   bias=m.b1eff[0:n, layer, NCH + c:NCH + c + 1]).then_inc(gelu_sb, 1)
                    if c == 0 and g + 1 < GROUPS:
                        leading(g + 1)
            if upcoming:
                Attention.first_step(upcoming.scalar(act))

        @block.vector
        def _(dve):
            vec = nc.vector

            def remainder(g):
                dve.wait_ge(turn_hi, g + 1)
                vec.tensor_tensor(hT[1][:, g % 2, :], m.bank[:, PT, :], hT[0][:, g % 2, :].bitcast(F32),
                                  ALU.subtract).then_inc(turn_lo, 1)

            def add_output(g):
                dve.wait_ge(down_mm, g + 1)
                for k in range(2):
                    rows = slice(k * HALF, (k + 1) * HALF)
                    r = m.res[rows, GSEQ * g:GSEQ * (g + 1), k:k + TOK]
                    last = vec.scalar_tensor_tensor(
                        out=r, in0=m.bank[rows, PD[g % 2], :].rearrange("p (s t) -> p s t", s=GSEQ),
                        scalar=m.cols[rows, 2, layer:layer + 1], in1=r, op0=ALU.add, op1=ALU.add)
                last.then_inc(res_ok, 1)

            def gates(g):
                for c, (_, n) in enumerate(CHUNKS):
                    n_chunk = NCH * g + c
                    dve.wait_ge(gelu_sb, n_chunk + 1)
                    at_least(dve, down_mm, g - 1)
                    vec.scalar_tensor_tensor(out=u[0:n, g % 2, c, :], in0=m.bank[0:n, PU[n_chunk % 2], :],
                                             scalar=m.b1eff[0:n, layer, c:c + 1], in1=gelu[0:n, n_chunk % 2, :],
                                             op0=ALU.add, op1=ALU.mult).then_inc(gate_sb, 1)
                    if c == 0 and g + 1 < GROUPS:
                        remainder(g + 1)
                    yield

            chain = Chain(dve, steps_sem, 0)
            remainder(0)
            for g in PR:
                dve.wait_ge(rows_mm, g - 1)
                row_stats(vec, chain, group_rows(m, PR[g]), m.stats[:, GSEQ * g:GSEQ * (g + 1), :])
            first = gates(0)
            next(first)
            pair_deviation(vec, chain, m, 2, first)
            for g in PR:
                normalise_rows(vec, m, g, PR[g]).then_inc(norm_ok, 1)
            for g in range(1, GROUPS - 1):
                for _ in gates(g):
                    pass
                add_output(g - 1)
            if upcoming:
                upcoming.split_lo(dve)
            last = gates(GROUPS - 1)
            next(last)
            add_output(GROUPS - 2)
            for _ in last:
                pass
            if upcoming:
                Attention.first_step(upcoming.vector(dve))
            add_output(GROUPS - 1)


def ternary_mlp(nc, m, a, out):
    with ExitStack() as ctx:
        sem = lambda name: ctx.enter_context(nc.semaphore(name))
        sb = lambda name, shape, dt=F32: ctx.enter_context(nc.sbuf_tensor(name, shape, dt))
        x1_ok, cond_mm, cond_hi, cond_lo, fc_mm, gelu_sb, norm_dve, coef_ready, norm_act = (
            sem(s) for s in ("l_x1_ok", "l_cond_mm", "l_cond_hi", "l_cond_lo", "l_fc_mm",
                             "l_gelu_sb", "l_norm_dve", "l_coef_ready", "l_norm_act"))
        turn_mm, turn_hi, turn_lo, bias_mm, proj_mm, sum_ok, back_mm, back_sb, steps_sem = (
            sem(s) for s in ("l_turn_mm", "l_turn_hi", "l_turn_lo", "l_bias_mm", "l_proj_mm", "l_sum_ok",
                             "l_back_mm", "l_back_sb", "l_steps"))
        stored = [sem(f"l_stored{half}") for half in range(2)]
        cT = [sb(f"l_cT_{k}", [P, SEQS, TOK], F32R) for k in ("hi", "lo")]
        gl = sb("l_gl", [P, SEQS, FC])
        gT = [sb(f"l_gT_{k}", [P, FC // P, GTOK], F32R) for k in ("hi", "lo")]
        proj_bias = sb("l_proj_bias", [P, 1])
        oT = sb("l_oT", [P, 2, GTOK])
        o = gl[:, 0:2, :]
        stats = sb("l_stats", [P, SEQS, 6])
        mv = sb("l_mv", [P, SEQS, 2])
        ve = sb("l_ve", [P, SEQS])
        rstd = sb("l_rstd", [P, SEQS])
        tmp = sb("l_tmp", [P, SEQS])
        last_group = GROUPS - 1
        BY_ACT = GSEQ // 2
        offset = sb("l_offset", [P, SEQS])
        PC, PF = (0, 7, 3, 4), (1, 2, 5, 6)
        PT, PP, PB, PBIAS = (3, 4, 1, 2), (5, 0), 6, 7
        block = ctx.enter_context(nc.Block())

        def seqs(g):
            return slice(GSEQ * g, GSEQ * (g + 1))

        @block.sync
        def _(sp):
            for g in range(GROUPS):
                sp.wait_ge(back_sb, g + 1)
                sp.dma_start(out[seqs(g), :, :].rearrange("s t d -> t s d"),
                             o[:, g % 2, :].rearrange("p (s d) -> p s d", s=GSEQ)).then_inc(stored[g % 2], 16)
            for half in stored:
                sp.wait_ge(half, 16 * GROUPS // 2)

        @block.tensor
        def _(pe):
            def up(g):
                if g == last_group:
                    pe.wait_ge(x1_ok, 1)
                for j in range(GSEQ):
                    mm = pe.matmul(m.bank[:, PC[g], j * P:(j + 1) * P], m.cwc[:, GSEQ * g + j, 0:DIM],
                                   m.x1T[:, GSEQ * g + j, :], start=True, stop=True)
                mm.then_inc(cond_mm, 1)

            def fc(g):
                for s in range(GSEQ * g, GSEQ * (g + 1)):
                    pe.wait_ge(cond_lo, s + 1)
                    at_least(pe, gelu_sb, s + 1 - len(PF))
                    bank = m.bank[:, PF[s % len(PF)], :]
                    pe.matmul(bank, cT[0][:, s, :], m.wfT[:, :], start=True, stop=False)
                    pe.matmul(bank, cT[1][:, s, :], m.wfT[:, :], start=False, stop=True)\
                        .then_inc(fc_mm, 1)

            def turn(g, c):
                pe.wait_ge(norm_dve, g + 1)
                pe.wait_ge(norm_act, g + 1)
                at_least(pe, turn_lo, 4 * g + c + 1 - len(PT))
                for j in range(GSEQ):
                    mm = pe.transpose(m.bank[:, PT[c], j * P:(j + 1) * P],
                                      gl[:, GSEQ * g + j, c * P:(c + 1) * P], m.ident[:, :])
                mm.then_inc(turn_mm, 1)

            def down(g, c):
                if c == 0:
                    at_least(pe, sum_ok, g - 1)
                pe.wait_ge(turn_lo, 4 * g + c + 1)
                bank = m.bank[:, PP[g % 2], :]
                pe.matmul(bank, m.wpT[:, c, :], gT[0][:, c, :], start=(c == 0), stop=False)
                pe.matmul(bank, m.wpT[:, c, :], gT[1][:, c, :], start=False, stop=(c == 3)).then_inc(proj_mm, 1)

            def back(g):
                pe.wait_ge(sum_ok, g + 1)
                at_least(pe, back_sb, g)
                for j in range(GSEQ):
                    mm = pe.transpose(m.bank[:, PB, j * P:(j + 1) * P], oT[:, g % 2, j * P:(j + 1) * P],
                                      m.ident[:, :])
                mm.then_inc(back_mm, 1)

            for g in range(GROUPS):
                up(g)
            for g in range(GROUPS):
                fc(g)
            for c in range(4):
                mm = pe.matmul(m.bank[:, PBIAS, 0:1], m.wpT[:, c, :].bitcast(F32), m.ln1[:, 1, c:c + 1],
                               start=(c == 0), stop=(c == 3))
            mm.then_inc(bias_mm, 1)
            for c in range(4):
                turn(0, c)
            pe.wait_ge(gelu_sb, SEQS)
            for g in range(GROUPS):
                for c in range(4):
                    if g < last_group:
                        turn(g + 1, c)
                    down(g, c)
                    if c == 1 and g > 0:
                        back(g - 1)
            back(last_group)

        @block.scalar
        def _(act):
            def leading(g):
                act.wait_ge(cond_mm, g + 1)
                for j in range(GSEQ):
                    s = GSEQ * g + j
                    last = act.activation(cT[0][:, s, :], m.bank[:, PC[g], j * P:(j + 1) * P], ACT.Identity,
                                          bias=m.cwc[:, s, DIM:DIM + 1])
                last.then_inc(cond_hi, 1)

            def gelu(g):
                for j in range(GSEQ):
                    act.wait_ge(fc_mm, GSEQ * g + j + 1)
                    act.activation(gl[:, GSEQ * g + j, :], m.bank[:, PF[j % len(PF)], :], ACT.Gelu).then_inc(gelu_sb, 1)

            def scaled_leading(g, c):
                act.wait_ge(turn_mm, 4 * g + c + 1)
                at_least(act, proj_mm, 4 * (g - 1) + c + 1)
                act.activation(gT[0][:, c, :], m.bank[:, PT[c], :], ACT.Identity,
                               scale=m.ln1[:, 0, c:c + 1]).then_inc(turn_hi, 1)

            def normalise(g):
                act.wait_ge(coef_ready, g // 2 + 1)
                for s in range(GSEQ * (g + 1) - BY_ACT, GSEQ * (g + 1)):
                    last = act.activation(gl[:, s, :], gl[:, s, :], ACT.Identity,
                                          scale=rstd[:, s:s + 1], bias=offset[:, s:s + 1])
                last.then_inc(norm_act, 1)

            def output(g):
                act.wait_ge(back_mm, g + 1)
                at_least(act, stored[g % 2], 16 * (g // 2))
                act.copy(o[:, g % 2, :], m.bank[:, PB, :]).then_inc(back_sb, 1)

            leading(0)
            leading(1)
            gelu(0)
            leading(2)
            gelu(1)
            leading(3)
            gelu(2)
            gelu(3)
            normalise(0)
            normalise(1)
            for g in range(GROUPS):
                for c in range(4):
                    scaled_leading(g, c)
                    if c == 1 and 0 < g < last_group:
                        normalise(g + 1)
                    if c == 2 and g > 1:
                        output(g - 2)
            output(last_group - 1)
            output(last_group)

        @block.vector
        def _(dve):
            vec = nc.vector
            chain = Chain(dve, steps_sem, 0)

            def remainder(g):
                dve.wait_ge(cond_hi, g + 1)
                for j in range(GSEQ):
                    s = GSEQ * g + j
                    vec.scalar_tensor_tensor(
                        out=cT[1][:, s, :], in0=m.bank[:, PC[g], j * P:(j + 1) * P],
                        scalar=m.cwc[:, s, DIM:DIM + 1], in1=cT[0][:, s, :].bitcast(F32),
                        op0=ALU.add, op1=ALU.subtract).then_inc(cond_lo, 1)

            def statistics(g):
                for s in range(GSEQ * g, GSEQ * (g + 1)):
                    dve.wait_ge(gelu_sb, s + 1)
                    row_stats(vec, chain, gl[:, s:s + 1, :], stats[:, s:s + 1, :])
                    yield

            def coefficients(g, between=iter(())):
                s = slice(GSEQ * g, GSEQ * (g + 2))
                inverse_deviation(vec, chain, stats[:, s, :], mv[:, s, :], ve[:, s], rstd[:, s], tmp[:, s], FC,
                                  between)
                vec.scalar_tensor_tensor(out=offset[:, s], in0=mv[:, s, 0], scalar=-1.0, in1=rstd[:, s],
                                         op0=ALU.mult, op1=ALU.mult).then_inc(coef_ready, 1)

            def normalise(g):
                count = GSEQ - BY_ACT
                for s in range(GSEQ * g, GSEQ * g + count):
                    last = vec.tensor_scalar(gl[:, s, :], gl[:, s, :], mv[:, s, 0:1], rstd[:, s:s + 1],
                                             ALU.subtract, ALU.mult)
                    if s == GSEQ * g + count - 1:
                        last.then_inc(norm_dve, 1)
                    yield

            def scaled_remainder(g, c):
                dve.wait_ge(turn_hi, 4 * g + c + 1)
                vec.scalar_tensor_tensor(out=gT[1][:, c, :], in0=m.bank[:, PT[c], :], scalar=m.ln1[:, 0, c:c + 1],
                                         in1=gT[0][:, c, :].bitcast(F32), op0=ALU.mult, op1=ALU.subtract)\
                    .then_inc(turn_lo, 1)

            def add_projection(g):
                dve.wait_ge(proj_mm, 4 * (g + 1))
                at_least(dve, back_mm, g - 1)
                vec.scalar_tensor_tensor(out=oT[:, g % 2, :], in0=m.bank[:, PP[g % 2], :], scalar=proj_bias[:, :],
                                         in1=m.x1T[:, seqs(g), :].rearrange("p s t -> p (s t)"),
                                         op0=ALU.add, op1=ALU.add).then_inc(sum_ok, 1)

            add_x(vec, m, last_group).then_inc(x1_ok, 1)
            remainder(0)
            remainder(1)
            complete(statistics(0))
            remainder(2)
            complete(statistics(1))

            def remainder_and_statistics():
                yield remainder(3)
                yield from statistics(2)

            coefficients(0, remainder_and_statistics())
            complete(normalise(0))
            complete(statistics(3))
            dve.wait_ge(bias_mm, 1)
            chain.add(vec.tensor_copy(proj_bias[:, :], m.bank[:, PBIAS, 0:1]))

            def normalise_and_remainder():
                yield from normalise(1)
                for c in range(4):
                    yield scaled_remainder(0, c)

            coefficients(2, normalise_and_remainder())
            complete(normalise(2))
            for g in range(1, GROUPS):
                for c in range(4):
                    scaled_remainder(g, c)
                    if c == 1:
                        add_projection(g - 1)
                if g + 2 < GROUPS:
                    complete(normalise(g + 2))
            add_projection(last_group)


def program(nc, a, out):
    with ExitStack() as ctx:
        m = Memory(nc, ctx)
        ffn_sems = StageSemaphores(nc, ctx)
        with ExitStack() as layers:
            buf = AttentionBuffers(nc, layers)
            attentions = [Attention(nc, layers, m, buf, layer) for layer in range(DEPTH)]
            prepare_and_adapt(nc, m, a, attentions[0])
            for layer in range(DEPTH):
                attentions[layer].run(nc, m, a, ffn_sems)
                gated_ffn(nc, m, layer, ffn_sems, attentions[layer + 1] if layer + 1 < DEPTH else None)
        ternary_mlp(nc, m, a, out)


def shape_constants():
    i, j = np.arange(TOK)[:, None], np.arange(TOK)[None, :]
    masked = (i < j) | (i > j + WINDOW)
    mask = np.where(masked, -1e30, 0.0).astype(np.float32)
    half = np.arange(0, HD, 2, dtype=np.float32)
    inv_freq = (1.0 / np.float32(10000.0) ** (half / HD)).astype(np.float32)
    t = np.arange(TOK, dtype=np.float32)
    freqs = (t[:, None] * inv_freq[None, :]).astype(np.float32)
    base = ((half + 0.4 * HD) / (1.4 * HD)).astype(np.float32)
    power = ((t - TOK // 2) / float(WINDOW // 2)).astype(np.float32)
    xpos = (base[None, :] ** power[:, None]).astype(np.float32)
    two = lambda z: np.concatenate([z, z], axis=-1)
    cos, sin, xpos = two(np.cos(freqs)), two(np.sin(freqs)), two(xpos)
    sin = sin * np.where(np.arange(HD) < HD // 2, 1.0, -1.0)
    rope = np.stack([np.stack([cos * xpos, cos / xpos], 1), np.stack([sin * xpos, sin / xpos], 1)], 1)
    return {
        "ident": np.eye(P, dtype=np.float32),
        "mask": mask,
        "rope": rope.astype(np.float32),
    }


def kernel(**inputs):
    import concourse.bacc as bacc
    from concourse.bass_utils import run_bass_kernel_spmd

    x = {k: np.asarray(v) for k, v in inputs.items()}
    cond = np.zeros((x["L0_cond_W1"].shape[0], P, COND), np.float32)
    cond[:, :, 0:ADIM] = x["L0_cond_W1"]
    cond[:, 0:ADIM, W2_AT:W2_AT + DIM] = x["L0_cond_W2"]
    cond[:, ADIM, W2_AT:W2_AT + DIM] = x["L0_cond_b2"]
    cond[:, :, GAMMA_AT] = x["L0_cond_gamma"]
    cond[:, :, BETA_AT] = x["L0_cond_beta"]
    cond[:, 0:ADIM, B1_AT] = x["L0_cond_b1"]
    arrays = {
        "x": x["x"], "idx": np.stack([x["itok_B_0_8"], x["itok_B_0_15"]]), "cond": cond,
        "cwc": np.concatenate([x["L1_cond_weights"], x["L1_cond_b"][:, :, None]], axis=2),
        "wqkv": x["L0_ffn_wqkv"], "wo": x["L0_ffn_wo"], "w1": x["L0_ffn_w1"], "w2": x["L0_ffn_w2"],
        "b1": x["L0_ffn_b1"], "b2": x["L0_ffn_b2"], "ln_g0": x["L0_ffn_ln_g"], "ln_b0": x["L0_ffn_ln_b"],
        "qks": np.stack([x["L0_ffn_q_scale"], x["L0_ffn_k_scale"]], axis=1).reshape(-1),
        "W_fc": x["L1_ffn_W_fc"], "W_proj": x["L1_ffn_W_proj"], "ln_w": x["L1_ffn_ln_w"], "ln_b": x["L1_ffn_ln_b"],
    }
    arrays |= shape_constants()
    nc = bacc.Bacc("TRN2", target_bir_lowering=False, num_devices=1)
    feed, aps = {}, {}
    for name, value in arrays.items():
        value = np.ascontiguousarray(value)
        feed[f"in_{name}"] = value
        aps[name] = nc.dram_tensor(f"in_{name}", value.shape, mybir.dt.from_np(value.dtype),
                                   kind="ExternalInput").ap()
    out = nc.dram_tensor("out_0", (SEQS, TOK, DIM), F32, kind="ExternalOutput").ap()
    program(nc, aps, out)
    return run_bass_kernel_spmd(nc, [feed], core_ids=[0]).results[0]["out_0"]
```
